# Optimizing a Trainium2 kernel written in Bass

```python
import numpy as np
import jax
import jax.numpy as jnp

def _softmax(x, axis=-1):
    return jax.nn.softmax(x, axis=axis)

def _gelu(x):
    return jax.nn.gelu(x, approximate=True)

def _silu(x):
    return jax.nn.silu(x)

def _sigmoid(x):
    return jax.nn.sigmoid(x)

def _layernorm(x, axis=-1, eps=1e-05):
    m = jnp.mean(x, axis=axis, keepdims=True)
    v = jnp.var(x, axis=axis, keepdims=True)
    return (x - m) / jnp.sqrt(v + eps)

def _scatter_add(tgt, idx, src, axis=0):
    return tgt.at[idx].add(src)

def _segment_sum(src, seg, n):
    return jax.ops.segment_sum(src, seg, n)
kernel_name = 'mk_pixart_seq_d4_seqx_r8_3824c5'

def setup_inputs(seed: int=0):
    np.random.seed(seed)
    _w = jnp.asarray

    def _rec_inputs():
        import jax
        import jax.numpy as jnp
        _rk = jax.random.key(seed)
        x = -0.0002928 + 1 * jax.random.normal(jax.random.fold_in(_rk, 1), (16, 256, 128), jnp.float32)
        _lenS = 256 - jax.random.randint(jax.random.fold_in(_rk, 7), (16,), 0, max(1, 256 // 4) + 1, jnp.int32)
        _lenS2 = 1601 - jax.random.randint(jax.random.fold_in(_rk, 8), (16,), 0, max(1, 1601 // 4) + 1, jnp.int32)
        cond_1024 = 0.0061147 + 1.02565 * jax.random.normal(jax.random.fold_in(_rk, 11), (16, 128), jnp.float32)
        _ctx_1024P = jax.random.normal(jax.random.fold_in(_rk, 12), (16, 16, 128), jnp.float32)
        _ctx_1024c = jax.random.dirichlet(jax.random.fold_in(_rk, 512), 0.3 * jnp.ones((16,), jnp.float32), (16, 1601))
        _ctx_1024t = jnp.einsum('bsk,bkd->bsd', _ctx_1024c, _ctx_1024P)
        _ctx_1024t = _ctx_1024t * jax.lax.rsqrt(jnp.mean(jnp.square(_ctx_1024t)) + 1e-12) * 0.953939
        ctx_1024 = -0.00265004 + 0.998804 * (_ctx_1024t + 0.3 * jax.random.normal(jax.random.fold_in(_rk, 612), (16, 1601, 128), jnp.float32))
        return (x, cond_1024, ctx_1024)
    x, cond_1024, ctx_1024 = _rec_inputs()

    def _L0_xcond_setup():
        import jax, jax.numpy as jnp
        import numpy as np
        LN_EPS = 1e-06

        def _ln(x):
            mu = jnp.mean(x, axis=-1, keepdims=True)
            var = jnp.var(x, axis=-1, keepdims=True)
            return (x - mu) * jax.lax.rsqrt(var + LN_EPS)
        key = jax.random.key(seed)
        H, NH = (128, 16)
        B, N, S = (4, 128, 77)
        MLP = int(H * 4.0)
        ks = jax.random.split(key, 20)
        s = 1.0 / np.sqrt(H)
        return {'x': jax.random.normal(ks[0], (B, N, H), jnp.float32), 'c': jax.random.normal(ks[1], (B, H), jnp.float32), 'context': jax.random.normal(ks[2], (B, S, H), jnp.float32), 'W_mod': jax.random.normal(ks[3], (H, 6 * H), jnp.float32) * s, 'b_mod': jnp.zeros((6 * H,), jnp.float32), 'W_qkv': jax.random.normal(ks[4], (H, 3 * H), jnp.float32) * s, 'b_qkv': jnp.zeros((3 * H,), jnp.float32), 'W_proj': jax.random.normal(ks[5], (H, H), jnp.float32) * s, 'b_proj': jnp.zeros((H,), jnp.float32), 'W_qc': jax.random.normal(ks[6], (H, H), jnp.float32) * s, 'b_qc': jnp.zeros((H,), jnp.float32), 'W_kvc': jax.random.normal(ks[7], (H, 2 * H), jnp.float32) * s, 'b_kvc': jnp.zeros((2 * H,), jnp.float32), 'W_cproj': jax.random.normal(ks[8], (H, H), jnp.float32) * s, 'b_cproj': jnp.zeros((H,), jnp.float32), 'W_mlp1': jax.random.normal(ks[9], (H, MLP), jnp.float32) * s, 'b_mlp1': jnp.zeros((MLP,), jnp.float32), 'W_mlp2': jax.random.normal(ks[10], (MLP, H), jnp.float32) * (1.0 / np.sqrt(MLP)), 'b_mlp2': jnp.zeros((H,), jnp.float32)}
    _L0_xcond_all = _L0_xcond_setup()
    _L0_xcond_in = {k: v for k, v in _L0_xcond_all.items() if k in ('W_mod', 'b_mod', 'W_qkv', 'b_qkv', 'W_proj', 'b_proj', 'W_qc', 'b_qc', 'W_kvc', 'b_kvc', 'W_cproj', 'b_cproj', 'W_mlp1', 'b_mlp1', 'W_mlp2', 'b_mlp2')}
    del _L0_xcond_all

    def _L1_xcond_setup():
        import jax, jax.numpy as jnp
        import numpy as np
        H = 128
        RH = 2 * H
        E = 3
        B, T, P = (8, 256, 64)
        LN_EPS = 1e-05

        def _layer_norm(x, gamma, beta):
            mu = jnp.mean(x, axis=-1, keepdims=True)
            var = jnp.mean(jnp.square(x - mu), axis=-1, keepdims=True)
            return (x - mu) * jax.lax.rsqrt(var + LN_EPS) * gamma + beta
        key = jax.random.key(seed)
        ks = jax.random.split(key, 24)
        s = lambda fan_in: 1.0 / np.sqrt(fan_in)
        inp = {'mix_hidden_states': jax.random.normal(ks[0], (B, T, H), jnp.float32), 'global_anchor': jax.random.normal(ks[1], (B, H), jnp.float32), 'prototype_bank': jax.random.normal(ks[2], (B, P, H), jnp.float32), 'ln_gamma': jnp.ones((H,), jnp.float32), 'ln_beta': jnp.zeros((H,), jnp.float32), 'Wq': jax.random.normal(ks[3], (H, H), jnp.float32) * s(H), 'Wk': jax.random.normal(ks[4], (H, H), jnp.float32) * s(H), 'Wv': jax.random.normal(ks[5], (H, H), jnp.float32) * s(H), 'router_W': jax.random.normal(ks[6], (3 * H, E), jnp.float32) * s(3 * H), 'router_b': jnp.zeros((E,), jnp.float32), 'e_w1': jax.random.normal(ks[7], (E, 3 * H, RH), jnp.float32) * s(3 * H), 'e_b1': jnp.zeros((E, RH), jnp.float32), 'e_w2': jax.random.normal(ks[8], (E, RH, H), jnp.float32) * s(RH), 'e_b2': jnp.zeros((E, H), jnp.float32), 'gate_w1': jax.random.normal(ks[9], (3 * H, H), jnp.float32) * s(3 * H), 'gate_b1': jnp.zeros((H,), jnp.float32), 'gate_w2': jax.random.normal(ks[10], (H, H), jnp.float32) * s(H), 'gate_b2': jnp.zeros((H,), jnp.float32), 'out_w': jax.random.normal(ks[11], (H, H), jnp.float32) * s(H), 'out_b': jnp.zeros((H,), jnp.float32)}
        return inp
    _L1_xcond_all = _L1_xcond_setup()
    _L1_xcond_in = {k: v for k, v in _L1_xcond_all.items() if k in ('ln_gamma', 'ln_beta', 'Wq', 'Wk', 'Wv', 'router_W', 'router_b', 'e_w1', 'e_b1', 'e_w2', 'e_b2', 'gate_w1', 'gate_b1', 'gate_w2', 'gate_b2', 'out_w', 'out_b')}
    del _L1_xcond_all

    def _L2_xcond_setup():
        import jax, jax.numpy as jnp
        import numpy as np
        EPS = 1e-05

        def _ada_ln(x, c, W_ss, b_ss):
            mu = jnp.mean(x, axis=-1, keepdims=True)
            var = jnp.mean((x - mu) ** 2, axis=-1, keepdims=True)
            h = (x - mu) / jnp.sqrt(var + EPS)
            ss = jax.nn.silu(c) @ W_ss + b_ss
            scale, bias = jnp.split(ss, 2, axis=-1)
            return (1.0 + scale)[:, None, :] * h + bias[:, None, :]
        key = jax.random.key(seed)
        ks = jax.random.split(key, 12)
        B, Lq, Lkv, H = (8, 256, 64, 128)
        s = 0.02
        return {'x_q': jax.random.normal(ks[0], (B, Lq, H), jnp.float32), 'x_kv': jax.random.normal(ks[1], (B, Lkv, H), jnp.float32), 't_vec': jax.random.normal(ks[2], (B, H), jnp.float32), 'Wq': jax.random.normal(ks[3], (H, H), jnp.float32) * s, 'bq': jnp.zeros((H,), jnp.float32), 'Wkv': jax.random.normal(ks[4], (H, 2 * H), jnp.float32) * s, 'bkv': jnp.zeros((2 * H,), jnp.float32), 'Wp': jax.random.normal(ks[5], (H, H), jnp.float32) * s, 'bp': jnp.zeros((H,), jnp.float32), 'Wss_q': jax.random.normal(ks[6], (H, 2 * H), jnp.float32) * s, 'bss_q': jnp.zeros((2 * H,), jnp.float32), 'Wss_kv': jax.random.normal(ks[7], (H, 2 * H), jnp.float32) * s, 'bss_kv': jnp.zeros((2 * H,), jnp.float32)}
    _L2_xcond_all = _L2_xcond_setup()
    _L2_xcond_in = {k: v for k, v in _L2_xcond_all.items() if k in ('Wq', 'bq', 'Wkv', 'bkv', 'Wp', 'bp', 'Wss_q', 'bss_q', 'Wss_kv', 'bss_kv')}
    del _L2_xcond_all

    def _L3_xcond_setup():
        import jax, jax.numpy as jnp
        import numpy as np
        D = 128
        H = 16
        HD = D // H
        MLP = 4 * D
        EPS = 1e-06
        SCALE = HD ** (-0.5)

        def _p(key, shape, s=0.02):
            return jax.random.normal(key, shape, dtype=jnp.float32) * s

        def _ln(x):
            mu = jnp.mean(x, axis=-1, keepdims=True)
            var = jnp.var(x, axis=-1, keepdims=True)
            return (x - mu) * jax.lax.rsqrt(var + EPS)

        def _heads(t):
            B, L, _ = t.shape
            return t.reshape(B, L, H, HD).transpose(0, 2, 1, 3)

        def _attend(q, k, v):
            attn = jnp.einsum('bhnd,bhsd->bhns', q, k) * SCALE
            attn = jax.nn.softmax(attn, axis=-1)
            o = jnp.einsum('bhns,bhsd->bhnd', attn, v)
            B, _, N, _ = q.shape
            return o.transpose(0, 2, 1, 3).reshape(B, N, D)
        key = jax.random.key(seed)
        ks = jax.random.split(key, 24)
        B, N, S = (4, 128, 77)
        return {'x': jax.random.normal(ks[0], (B, N, D), dtype=jnp.float32), 't_emb': jax.random.normal(ks[1], (B, D), dtype=jnp.float32), 'context': jax.random.normal(ks[2], (B, S, D), dtype=jnp.float32), 'adaln_w': _p(ks[3], (D, 6 * D)), 'adaln_b': _p(ks[4], (6 * D,)), 'qkv_w': _p(ks[5], (D, 3 * D)), 'qkv_b': _p(ks[6], (3 * D,)), 'sa_proj_w': _p(ks[7], (D, D)), 'sa_proj_b': _p(ks[8], (D,)), 'q_w': _p(ks[9], (D, D)), 'q_b': _p(ks[10], (D,)), 'kv_w': _p(ks[11], (D, 2 * D)), 'kv_b': _p(ks[12], (2 * D,)), 'ca_proj_w': _p(ks[13], (D, D)), 'ca_proj_b': _p(ks[14], (D,)), 'fc1_w': _p(ks[15], (D, MLP)), 'fc1_b': _p(ks[16], (MLP,)), 'fc2_w': _p(ks[17], (MLP, D)), 'fc2_b': _p(ks[18], (D,))}
    _L3_xcond_all = _L3_xcond_setup()
    _L3_xcond_in = {k: v for k, v in _L3_xcond_all.items() if k in ('adaln_w', 'adaln_b', 'qkv_w', 'qkv_b', 'sa_proj_w', 'sa_proj_b', 'q_w', 'q_b', 'kv_w', 'kv_b', 'ca_proj_w', 'ca_proj_b', 'fc1_w', 'fc1_b', 'fc2_w', 'fc2_b')}
    del _L3_xcond_all
    return {'x': x, 'cond_1024': cond_1024, 'ctx_1024': ctx_1024, 'L0_xcond_W_mod': _L0_xcond_in['W_mod'], 'L0_xcond_b_mod': _L0_xcond_in['b_mod'], 'L0_xcond_W_qkv': _L0_xcond_in['W_qkv'], 'L0_xcond_b_qkv': _L0_xcond_in['b_qkv'], 'L0_xcond_W_proj': _L0_xcond_in['W_proj'], 'L0_xcond_b_proj': _L0_xcond_in['b_proj'], 'L0_xcond_W_qc': _L0_xcond_in['W_qc'], 'L0_xcond_b_qc': _L0_xcond_in['b_qc'], 'L0_xcond_W_kvc': _L0_xcond_in['W_kvc'], 'L0_xcond_b_kvc': _L0_xcond_in['b_kvc'], 'L0_xcond_W_cproj': _L0_xcond_in['W_cproj'], 'L0_xcond_b_cproj': _L0_xcond_in['b_cproj'], 'L0_xcond_W_mlp1': _L0_xcond_in['W_mlp1'], 'L0_xcond_b_mlp1': _L0_xcond_in['b_mlp1'], 'L0_xcond_W_mlp2': _L0_xcond_in['W_mlp2'], 'L0_xcond_b_mlp2': _L0_xcond_in['b_mlp2'], 'L1_xcond_ln_gamma': _L1_xcond_in['ln_gamma'], 'L1_xcond_ln_beta': _L1_xcond_in['ln_beta'], 'L1_xcond_Wq': _L1_xcond_in['Wq'], 'L1_xcond_Wk': _L1_xcond_in['Wk'], 'L1_xcond_Wv': _L1_xcond_in['Wv'], 'L1_xcond_router_W': _L1_xcond_in['router_W'], 'L1_xcond_router_b': _L1_xcond_in['router_b'], 'L1_xcond_e_w1': _L1_xcond_in['e_w1'], 'L1_xcond_e_b1': _L1_xcond_in['e_b1'], 'L1_xcond_e_w2': _L1_xcond_in['e_w2'], 'L1_xcond_e_b2': _L1_xcond_in['e_b2'], 'L1_xcond_gate_w1': _L1_xcond_in['gate_w1'], 'L1_xcond_gate_b1': _L1_xcond_in['gate_b1'], 'L1_xcond_gate_w2': _L1_xcond_in['gate_w2'], 'L1_xcond_gate_b2': _L1_xcond_in['gate_b2'], 'L1_xcond_out_w': _L1_xcond_in['out_w'], 'L1_xcond_out_b': _L1_xcond_in['out_b'], 'L2_xcond_Wq': _L2_xcond_in['Wq'], 'L2_xcond_bq': _L2_xcond_in['bq'], 'L2_xcond_Wkv': _L2_xcond_in['Wkv'], 'L2_xcond_bkv': _L2_xcond_in['bkv'], 'L2_xcond_Wp': _L2_xcond_in['Wp'], 'L2_xcond_bp': _L2_xcond_in['bp'], 'L2_xcond_Wss_q': _L2_xcond_in['Wss_q'], 'L2_xcond_bss_q': _L2_xcond_in['bss_q'], 'L2_xcond_Wss_kv': _L2_xcond_in['Wss_kv'], 'L2_xcond_bss_kv': _L2_xcond_in['bss_kv'], 'L3_xcond_adaln_w': _L3_xcond_in['adaln_w'], 'L3_xcond_adaln_b': _L3_xcond_in['adaln_b'], 'L3_xcond_qkv_w': _L3_xcond_in['qkv_w'], 'L3_xcond_qkv_b': _L3_xcond_in['qkv_b'], 'L3_xcond_sa_proj_w': _L3_xcond_in['sa_proj_w'], 'L3_xcond_sa_proj_b': _L3_xcond_in['sa_proj_b'], 'L3_xcond_q_w': _L3_xcond_in['q_w'], 'L3_xcond_q_b': _L3_xcond_in['q_b'], 'L3_xcond_kv_w': _L3_xcond_in['kv_w'], 'L3_xcond_kv_b': _L3_xcond_in['kv_b'], 'L3_xcond_ca_proj_w': _L3_xcond_in['ca_proj_w'], 'L3_xcond_ca_proj_b': _L3_xcond_in['ca_proj_b'], 'L3_xcond_fc1_w': _L3_xcond_in['fc1_w'], 'L3_xcond_fc1_b': _L3_xcond_in['fc1_b'], 'L3_xcond_fc2_w': _L3_xcond_in['fc2_w'], 'L3_xcond_fc2_b': _L3_xcond_in['fc2_b']}

def reference(x, cond_1024, ctx_1024, L0_xcond_W_mod, L0_xcond_b_mod, L0_xcond_W_qkv, L0_xcond_b_qkv, L0_xcond_W_proj, L0_xcond_b_proj, L0_xcond_W_qc, L0_xcond_b_qc, L0_xcond_W_kvc, L0_xcond_b_kvc, L0_xcond_W_cproj, L0_xcond_b_cproj, L0_xcond_W_mlp1, L0_xcond_b_mlp1, L0_xcond_W_mlp2, L0_xcond_b_mlp2, L1_xcond_ln_gamma, L1_xcond_ln_beta, L1_xcond_Wq, L1_xcond_Wk, L1_xcond_Wv, L1_xcond_router_W, L1_xcond_router_b, L1_xcond_e_w1, L1_xcond_e_b1, L1_xcond_e_w2, L1_xcond_e_b2, L1_xcond_gate_w1, L1_xcond_gate_b1, L1_xcond_gate_w2, L1_xcond_gate_b2, L1_xcond_out_w, L1_xcond_out_b, L2_xcond_Wq, L2_xcond_bq, L2_xcond_Wkv, L2_xcond_bkv, L2_xcond_Wp, L2_xcond_bp, L2_xcond_Wss_q, L2_xcond_bss_q, L2_xcond_Wss_kv, L2_xcond_bss_kv, L3_xcond_adaln_w, L3_xcond_adaln_b, L3_xcond_qkv_w, L3_xcond_qkv_b, L3_xcond_sa_proj_w, L3_xcond_sa_proj_b, L3_xcond_q_w, L3_xcond_q_b, L3_xcond_kv_w, L3_xcond_kv_b, L3_xcond_ca_proj_w, L3_xcond_ca_proj_b, L3_xcond_fc1_w, L3_xcond_fc1_b, L3_xcond_fc2_w, L3_xcond_fc2_b):
    import jax
    import jax.numpy as jnp

    def _L0_xcond_ref(x, c, context, W_mod, b_mod, W_qkv, b_qkv, W_proj, b_proj, W_qc, b_qc, W_kvc, b_kvc, W_cproj, b_cproj, W_mlp1, b_mlp1, W_mlp2, b_mlp2):
        import jax, jax.numpy as jnp
        import numpy as np
        LN_EPS = 1e-06

        def _ln(x):
            mu = jnp.mean(x, axis=-1, keepdims=True)
            var = jnp.var(x, axis=-1, keepdims=True)
            return (x - mu) * jax.lax.rsqrt(var + LN_EPS)
        B, N, H = x.shape
        NH = 16
        hd = H // NH
        scale = hd ** (-0.5)
        c_proj = jax.nn.silu(c) @ W_mod + b_mod
        shift_a, scale_a, gate_a, shift_m, scale_m, gate_m = jnp.split(c_proj, 6, axis=-1)

        def modulate(t, shift, sc):
            return t * (1 + sc[:, None]) + shift[:, None]
        x_norm = modulate(_ln(x), shift_a, scale_a)
        qkv = x_norm @ W_qkv + b_qkv
        q, k, v = jnp.split(qkv, 3, axis=-1)
        q = q.reshape(B, N, NH, hd).transpose(0, 2, 1, 3)
        k = k.reshape(B, N, NH, hd).transpose(0, 2, 1, 3)
        v = v.reshape(B, N, NH, hd).transpose(0, 2, 1, 3)
        attn_w = jax.nn.softmax(jnp.einsum('bhqd,bhkd->bhqk', q, k) * scale, axis=-1)
        attn_out = jnp.einsum('bhqk,bhkd->bhqd', attn_w, v)
        attn_out = attn_out.transpose(0, 2, 1, 3).reshape(B, N, H)
        attn_out = attn_out @ W_proj + b_proj
        x = x + gate_a[:, None] * attn_out
        S = context.shape[1]
        q_c = _ln(x) @ W_qc + b_qc
        kv_c = _ln(context) @ W_kvc + b_kvc
        k_c, v_c = jnp.split(kv_c, 2, axis=-1)
        q_c = q_c.reshape(B, N, NH, hd).transpose(0, 2, 1, 3)
        k_c = k_c.reshape(B, S, NH, hd).transpose(0, 2, 1, 3)
        v_c = v_c.reshape(B, S, NH, hd).transpose(0, 2, 1, 3)
        c_attn_w = jax.nn.softmax(jnp.einsum('bhqd,bhsd->bhqs', q_c, k_c) * scale, axis=-1)
        c_attn_out = jnp.einsum('bhqs,bhsd->bhqd', c_attn_w, v_c)
        c_attn_out = c_attn_out.transpose(0, 2, 1, 3).reshape(B, N, H)
        c_attn_out = c_attn_out @ W_cproj + b_cproj
        x = x + c_attn_out
        x_norm2 = modulate(_ln(x), shift_m, scale_m)
        h = jax.nn.gelu(x_norm2 @ W_mlp1 + b_mlp1)
        h = h @ W_mlp2 + b_mlp2
        x = x + gate_m[:, None] * h
        return x

    def _L1_xcond_ref(mix_hidden_states, global_anchor, prototype_bank, ln_gamma, ln_beta, Wq, Wk, Wv, router_W, router_b, e_w1, e_b1, e_w2, e_b2, gate_w1, gate_b1, gate_w2, gate_b2, out_w, out_b):
        import jax, jax.numpy as jnp
        import numpy as np
        H = 128
        RH = 2 * H
        E = 3
        B, T, P = (8, 256, 64)
        LN_EPS = 1e-05

        def _layer_norm(x, gamma, beta):
            mu = jnp.mean(x, axis=-1, keepdims=True)
            var = jnp.mean(jnp.square(x - mu), axis=-1, keepdims=True)
            return (x - mu) * jax.lax.rsqrt(var + LN_EPS) * gamma + beta
        x = mix_hidden_states
        nx = _layer_norm(x, ln_gamma, ln_beta)
        q = nx @ Wq
        k = prototype_bank @ Wk
        v = prototype_bank @ Wv
        scores = jnp.einsum('bth,bph->btp', q, k) * H ** (-0.5)
        weights = jax.nn.softmax(scores, axis=-1)
        evidence = jnp.einsum('btp,bph->bth', weights, v)
        anchor = jnp.broadcast_to(global_anchor[:, None, :], nx.shape)
        combined = jnp.concatenate([nx, evidence, anchor], axis=-1)
        router_logits = combined @ router_W + router_b
        router_probs = jax.nn.softmax(router_logits, axis=-1)
        h = jax.nn.silu(jnp.einsum('btc,ecr->bter', combined, e_w1) + e_b1)
        expert_out = jnp.einsum('bter,erh->bteh', h, e_w2) + e_b2
        routed = jnp.sum(expert_out * router_probs[..., None], axis=-2)
        g = jax.nn.sigmoid(jax.nn.silu(combined @ gate_w1 + gate_b1) @ gate_w2 + gate_b2)
        refined_delta = g * (routed @ out_w + out_b)
        return x + refined_delta

    def _L2_xcond_ref(x_q, x_kv, t_vec, Wq, bq, Wkv, bkv, Wp, bp, Wss_q, bss_q, Wss_kv, bss_kv):
        import jax, jax.numpy as jnp
        import numpy as np
        EPS = 1e-05

        def _ada_ln(x, c, W_ss, b_ss):
            mu = jnp.mean(x, axis=-1, keepdims=True)
            var = jnp.mean((x - mu) ** 2, axis=-1, keepdims=True)
            h = (x - mu) / jnp.sqrt(var + EPS)
            ss = jax.nn.silu(c) @ W_ss + b_ss
            scale, bias = jnp.split(ss, 2, axis=-1)
            return (1.0 + scale)[:, None, :] * h + bias[:, None, :]
        B, Lq, H = x_q.shape
        Lkv = x_kv.shape[1]
        nh = 16
        dh = H // nh
        xq = _ada_ln(x_q, t_vec, Wss_q, bss_q)
        xkv = _ada_ln(x_kv, t_vec, Wss_kv, bss_kv)
        q = (xq @ Wq + bq).reshape(B, Lq, nh, dh)
        kv = (xkv @ Wkv + bkv).reshape(B, Lkv, 2, nh, dh)
        k = kv[:, :, 0]
        v = kv[:, :, 1]
        scores = jnp.einsum('bqhd,bkhd->bhqk', q, k) / jnp.sqrt(jnp.float32(dh))
        attn = jax.nn.softmax(scores, axis=-1)
        out = jnp.einsum('bhqk,bkhd->bqhd', attn, v).reshape(B, Lq, H)
        return x_q + (out @ Wp + bp)

    def _L3_xcond_ref(x, t_emb, context, adaln_w, adaln_b, qkv_w, qkv_b, sa_proj_w, sa_proj_b, q_w, q_b, kv_w, kv_b, ca_proj_w, ca_proj_b, fc1_w, fc1_b, fc2_w, fc2_b):
        import jax, jax.numpy as jnp
        import numpy as np
        D = 128
        H = 16
        HD = D // H
        MLP = 4 * D
        EPS = 1e-06
        SCALE = HD ** (-0.5)

        def _p(key, shape, s=0.02):
            return jax.random.normal(key, shape, dtype=jnp.float32) * s

        def _ln(x):
            mu = jnp.mean(x, axis=-1, keepdims=True)
            var = jnp.var(x, axis=-1, keepdims=True)
            return (x - mu) * jax.lax.rsqrt(var + EPS)

        def _heads(t):
            B, L, _ = t.shape
            return t.reshape(B, L, H, HD).transpose(0, 2, 1, 3)

        def _attend(q, k, v):
            attn = jnp.einsum('bhnd,bhsd->bhns', q, k) * SCALE
            attn = jax.nn.softmax(attn, axis=-1)
            o = jnp.einsum('bhns,bhsd->bhnd', attn, v)
            B, _, N, _ = q.shape
            return o.transpose(0, 2, 1, 3).reshape(B, N, D)
        B, N, _ = x.shape
        S = context.shape[1]
        mod = jax.nn.silu(t_emb) @ adaln_w + adaln_b
        sh_sa, sc_sa, g_sa, sh_ff, sc_ff, g_ff = jnp.split(mod[:, None, :], 6, axis=-1)
        xm = _ln(x) * (1.0 + sc_sa) + sh_sa
        qkv = (xm @ qkv_w + qkv_b).reshape(B, N, 3, H, HD)
        q = qkv[:, :, 0].transpose(0, 2, 1, 3)
        k = qkv[:, :, 1].transpose(0, 2, 1, 3)
        v = qkv[:, :, 2].transpose(0, 2, 1, 3)
        x_sa = _attend(q, k, v) @ sa_proj_w + sa_proj_b
        x = x + g_sa * x_sa
        xn = _ln(x)
        q = _heads(xn @ q_w + q_b)
        kv = (context @ kv_w + kv_b).reshape(B, S, 2, H, HD)
        k = kv[:, :, 0].transpose(0, 2, 1, 3)
        v = kv[:, :, 1].transpose(0, 2, 1, 3)
        x_ca = _attend(q, k, v) @ ca_proj_w + ca_proj_b
        x = x + x_ca
        xm = _ln(x) * (1.0 + sc_ff) + sh_ff
        h = jax.nn.gelu(xm @ fc1_w + fc1_b, approximate=True)
        x_ff = h @ fc2_w + fc2_b
        x = x + g_ff * x_ff
        return x
    x = _L0_xcond_ref(x, cond_1024, ctx_1024, L0_xcond_W_mod, L0_xcond_b_mod, L0_xcond_W_qkv, L0_xcond_b_qkv, L0_xcond_W_proj, L0_xcond_b_proj, L0_xcond_W_qc, L0_xcond_b_qc, L0_xcond_W_kvc, L0_xcond_b_kvc, L0_xcond_W_cproj, L0_xcond_b_cproj, L0_xcond_W_mlp1, L0_xcond_b_mlp1, L0_xcond_W_mlp2, L0_xcond_b_mlp2)
    x = _L1_xcond_ref(x, cond_1024, ctx_1024, L1_xcond_ln_gamma, L1_xcond_ln_beta, L1_xcond_Wq, L1_xcond_Wk, L1_xcond_Wv, L1_xcond_router_W, L1_xcond_router_b, L1_xcond_e_w1, L1_xcond_e_b1, L1_xcond_e_w2, L1_xcond_e_b2, L1_xcond_gate_w1, L1_xcond_gate_b1, L1_xcond_gate_w2, L1_xcond_gate_b2, L1_xcond_out_w, L1_xcond_out_b)
    x = _L2_xcond_ref(x, ctx_1024, cond_1024, L2_xcond_Wq, L2_xcond_bq, L2_xcond_Wkv, L2_xcond_bkv, L2_xcond_Wp, L2_xcond_bp, L2_xcond_Wss_q, L2_xcond_bss_q, L2_xcond_Wss_kv, L2_xcond_bss_kv)
    x = _L3_xcond_ref(x, cond_1024, ctx_1024, L3_xcond_adaln_w, L3_xcond_adaln_b, L3_xcond_qkv_w, L3_xcond_qkv_b, L3_xcond_sa_proj_w, L3_xcond_sa_proj_b, L3_xcond_q_w, L3_xcond_q_b, L3_xcond_kv_w, L3_xcond_kv_b, L3_xcond_ca_proj_w, L3_xcond_ca_proj_b, L3_xcond_fc1_w, L3_xcond_fc1_b, L3_xcond_fc2_w, L3_xcond_fc2_b)
    return x

_drawn_inputs = setup_inputs


def setup_inputs(seed=0):
    import zlib

    import numpy as np

    out = dict(_drawn_inputs(seed))
    spreads = {'L0_xcond_b_mod': (0.0, 0.1),
     'L0_xcond_b_qkv': (0.0, 0.1),
     'L0_xcond_b_proj': (0.0, 0.1),
     'L0_xcond_b_qc': (0.0, 0.539),
     'L0_xcond_b_kvc': (0.0, 0.1),
     'L0_xcond_b_cproj': (0.0, 0.1),
     'L0_xcond_b_mlp1': (0.0, 0.1),
     'L0_xcond_b_mlp2': (0.0, 0.1),
     'L1_xcond_ln_gamma': (1.0, 0.6),
     'L1_xcond_ln_beta': (0.0, 0.767),
     'L1_xcond_router_b': (0.0, 0.543),
     'L1_xcond_e_b1': (0.0, 0.507),
     'L1_xcond_e_b2': (0.0, 0.297),
     'L1_xcond_gate_b1': (0.0, 0.8),
     'L1_xcond_gate_b2': (0.0, 0.8),
     'L1_xcond_out_b': (0.0, 0.1),
     'L2_xcond_bq': (0.0, 0.8),
     'L2_xcond_bkv': (0.0, 0.423),
     'L2_xcond_bp': (0.0, 0.1),
     'L2_xcond_bss_q': (0.0, 0.8),
     'L2_xcond_bss_kv': (0.0, 0.8)}
    factors = {'L1_xcond_Wq': 2.705,
     'L1_xcond_Wk': 2.715,
     'L2_xcond_Wq': 8.0,
     'L2_xcond_Wkv': 2.761,
     'L2_xcond_Wss_q': 8.0,
     'L2_xcond_Wss_kv': 8.0,
     'L3_xcond_adaln_w': 8.0,
     'L3_xcond_adaln_b': 8.0,
     'L3_xcond_qkv_w': 8.0,
     'L3_xcond_qkv_b': 8.0,
     'L3_xcond_sa_proj_w': 8.0,
     'L3_xcond_sa_proj_b': 8.0,
     'L3_xcond_q_w': 33.81,
     'L3_xcond_q_b': 200.0,
     'L3_xcond_kv_w': 2.777,
     'L3_xcond_kv_b': 35.553,
     'L3_xcond_ca_proj_w': 2.831,
     'L3_xcond_ca_proj_b': 21.957,
     'L3_xcond_fc1_w': 8.0,
     'L3_xcond_fc1_b': 8.0,
     'L3_xcond_fc2_w': 8.0,
     'L3_xcond_fc2_b': 31.735}
    for name, (base, spread) in spreads.items():
        noise = np.random.default_rng([zlib.crc32(name.encode()), seed]).standard_normal(out[name].shape)
        drawn = base * np.exp(spread * noise) if base else spread * noise
        out[name] = jnp.asarray(drawn.astype(out[name].dtype))
    for name, factor in factors.items():
        out[name] = (out[name] * factor).astype(out[name].dtype)
    return out
```

```python
from contextlib import ExitStack

import concourse.bass as bass
from concourse import mybir

F32 = mybir.dt.float32
BF16 = mybir.dt.bfloat16
I32 = mybir.dt.int32
ALU = mybir.AluOpType
ACT = mybir.ActivationFunctionType
AX = mybir.AxisListType

P = 128
B = 16
NQ = 256
QT = NQ // P
S = 1601
D = 128
H = 16
HD = D // H
PAIRS = H // 2
QUADS = H // 4
ROWS = 64
MAX_ROW = 48
K_PART = (0, 0, 0, 1, 1, 2)
Q_PART = (0, 1, 2, 0, 1, 0)
RING_S = 3
RING_P = 4
MLP = 512
MC = MLP // P
GELU_SCALE, GELU_CUBE = 0.7978845608028654, 0.044715


def after(b, per, k):
    return b * per + k + 1


def wait(eng, sem, value):
    if isinstance(value, int) and value < 1:
        return
    eng.wait_ge(sem, value)


def wait_apart(eng, sem, value, met):
    if isinstance(value, int):
        wait(eng, sem, value)
        return
    value = eng.snap(eng.to_reg(value))
    eng.wait_ge(*met)
    eng.wait_ge(sem, value)


class Semaphores:

    def __init__(self, nc):
        self.nc, self.taken = nc, []

    def __enter__(self):
        return self

    def __call__(self, name):
        self.taken.append(self.nc.alloc_semaphore(name))
        return self.taken[-1]

    def __exit__(self, *_):
        self.nc.clear_and_free_semaphores(self.taken)
        self.nc.all_engine_barrier()


def column(t, c):
    return t[:, c:c + 1]


def has_before(b):
    return not (isinstance(b, int) and b == 0)


class Attention:

    def __init__(self, name, keys, x_src, x_dst, wq, wk, wv, wo, bq, bk, bv, bo, eps, ctx=None, ctx_ln=None,
                 q_cols=None, k_cols=None, gate=None, mlp=None):
        self.name, self.keys, self.x_src, self.x_dst = name, keys, x_src, x_dst
        self.wq, self.wk, self.wv, self.wo = wq, wk, wv, wo
        self.bq, self.bk, self.bv, self.bo = bq, bk, bv, bo
        self.eps = eps
        self.ctx = ctx
        self.ctx_ln = ctx_ln
        self.q_cols = q_cols
        self.k_cols = k_cols
        self.gate = gate
        self.mlp = mlp


def chunks_of(n, most):
    k = -(-n // most)
    out, at = [], 0
    for i in range(k):
        w = (n - at) // (k - i) + (1 if (n - at) % (k - i) else 0)
        out.append((at, w))
        at += w
    return out


class Chain:

    def __init__(self, eng, sem, base):
        self.eng, self.sem, self.base, self.n = eng, sem, base, 0

    def __call__(self, ins):
        ins.then_inc(self.sem, 1)
        self.n += 1

    def join(self):
        self.eng.wait_ge(self.sem, self.base + self.n)

    def join_apart(self, met):
        wait_apart(self.eng, self.sem, self.base + self.n, met)


RSQRT_STEPS = 3
RSQRT_LINKS = 3 + 4 * RSQRT_STEPS


def rsqrt(eng, link, spread, var, y, t, eps):
    link(eng.tensor_scalar(var, spread, eps, None, ALU.add))
    link.join()
    link(eng.tensor_scalar(t.bitcast(I32), var.bitcast(I32), 1, None, ALU.logical_shift_right))
    link.join()
    link(eng.tensor_scalar(y.bitcast(I32), t.bitcast(I32), -1, 0x5F3759DF, ALU.mult, ALU.add))
    link.join()
    for _ in range(RSQRT_STEPS):
        link(eng.tensor_tensor(t, y, y, ALU.mult))
        link.join()
        link(eng.tensor_tensor(t, t, var, ALU.mult))
        link.join()
        link(eng.tensor_scalar(t, t, -0.5, 1.5, ALU.mult, ALU.add))
        link.join()
        link(eng.tensor_tensor(y, y, t, ALU.mult))
        link.join()


def schedule(nb, keys, has_ctx, has_mlp):
    kt = -(-keys // P)
    slots = 8
    steps = [(q, t) for q in range(QUADS) for t in range(kt)]
    c_of = [[] for _ in range(slots)]
    for n, st in enumerate(steps):
        c_of[n * slots // len(steps)].append(("C",) + st)
    nch = len(chunks_of(keys, 512))

    def maxima(which, p):
        return [("M", which, p, a, qt, ch) for a in range(2) for qt in range(QT) for ch in range(nch)]

    m_of = [maxima(0, 6), maxima(0, 7), [("R", 0, 1)], maxima(1, 0), maxima(1, 1) + maxima(1, 2),
            maxima(1, 3) + maxima(1, 4), [("R", 1, 0)] + maxima(1, 5), []]
    if has_ctx:
        a_steps = ["ln", "ctx0", "ctx1", "k0", "k1", "ctx2", "ctx3", "k2", "k3", "ksplit", "xt", "q", "v0", "v1", "v2", "v3"]
        a_of = [a_steps[0:6], a_steps[6:11], a_steps[11:], [], [], [], [], []]
    else:
        a_steps = ["ln", "xt", "k0", "ksplit", "q", "v0"]
        a_of = [a_steps, [], [], [], [], [], [], []]
    d_of = [["o0"], ["o1"], ["ot"], ["proj"], [], [], [], []]
    if has_mlp:
        d_of = [["o0", "o1"], ["ot"], ["proj"], ["x2t"], ["h0"], ["h1"], ["fc2"], []]
    out = []
    for s in range(slots):
        lists = [m_of[s], [("A", k) for k in a_of[s]], [("D", k) for k in d_of[s]]]
        main = c_of[s] or []
        marks = []
        for kind in [main] + lists:
            marks += [((i + 0.5) / len(kind), i, st) for i, st in enumerate(kind)]
        marks.sort(key=lambda m: m[0])
        out += [st for _, _, st in marks]
    return out


def attention_layer(nc, spec, cols_d, rows_d, ident_d, nb):
    KEYS = spec.keys
    KT = -(-KEYS // P)
    LAST = KEYS - (KT - 1) * P
    CH = chunks_of(KEYS, 512)
    NCH = len(CH)
    JC = KT * PAIRS
    UP = 2 * QT * NCH
    UM = PAIRS * UP + 2
    has_ctx, mlp = spec.ctx is not None, spec.mlp
    TG = [(g, min(4, KT - g)) for g in range(0, KT, 4)]
    nm = spec.name
    K_EVACS = len(CH)
    A_USES = (len(TG) if has_ctx else 0) + 1 + NCH + 1 + len(TG)
    D_USES = 4 + (4 if mlp else 0)
    SCHED = schedule(nb, KEYS, has_ctx, bool(mlp))

    if has_ctx:
        a_order = [f"ctx{i}" for i in range(len(TG))]
        a_order = ["ctx0", "ctx1", "k0", "k1", "ctx2", "ctx3", "k2", "k3", "xt", "q", "v0", "v1", "v2", "v3"]
    else:
        a_order = ["xt", "k0", "q", "v0"]
    d_order = ["o0", "o1", "ot", "proj"] + (["x2t", "h0", "h1", "fc2"] if mlp else [])
    assert len(a_order) == A_USES and len(d_order) == D_USES

    with Semaphores(nc) as sems, ExitStack() as ctx:
        def sb(name, shape, dt=F32):
            return ctx.enter_context(nc.sbuf_tensor(f"{nm}_{name}", shape, dt))

        def sem(name):
            return sems(f"{nm}_{name}")

        def bank(name):
            return ctx.enter_context(nc.psum_tensor(f"{nm}_bank_{name}", [P, 512], F32))

        k_scr = nc.dram_tensor(f"{nm}_k_scr", (2, 3, 2, HD, PAIRS, KEYS), BF16, kind="Internal").ap()
        q_scr = nc.dram_tensor(f"{nm}_q_scr", (2, 3, 2, HD, PAIRS, NQ), BF16, kind="Internal").ap()
        m_scr = nc.dram_tensor(f"{nm}_m_scr", (2, 2, 2, 4, 2, NQ), BF16, kind="Internal").ap()

        ident = sb("ident", [P, P])
        wq, wk, wv, wo = (sb(n, [P, D]) for n in ("wq", "wk", "wv", "wo"))
        bq, bk = sb("bq", [P, 1]), sb("bk", [P, 1])
        bv = sb("bv", [P, 1])
        bo_rows = sb("bo_rows", [P, D])
        wqp, wkp = sb("wqp", [P, D]), sb("wkp", [P, D])
        zeros = sb("zeros", [2, PAIRS * NQ], BF16)
        xin = sb("xin", [P, QT, D])
        xres = sb("xres", [P, QT, D])
        NC = cols_d.shape[2]
        acols = sb("acols", [P, NC])
        gate = sb("gate", [P, D]) if spec.gate is not None else None
        stats = sb("stats", [P, QT, 6])
        agg = sb("agg", [P, QT, 2])
        rs_v, rs_y, rs_t = sb("rs_v", [P, QT]), sb("rs_y", [P, QT]), sb("rs_t", [P, QT])
        xn = sb("xn", [P, QT, D])
        xmt = sb("xmt", [P, NQ])
        qf, qr = sb("qf", [P, NQ]), sb("qr", [P, NQ])
        qsp = sb("qsp", [P, 3, NQ], BF16)
        kf, kr = sb("kf", [P, KEYS]), sb("kr", [P, KEYS])
        ksp = sb("ksp", [P, 3, KEYS], BF16)
        qst = [sb(f"qst{i}", [P, 2, PAIRS, NQ], BF16) for i in range(2)]
        kst = [sb(f"kst{i}", [P, PAIRS, KEYS], BF16) for i in range(2)]
        vaug = [sb(f"vaug{i}", [P, KT, H, HD + 1]) for i in range(2)]
        probs = [sb(f"probs{i}", [P, 512]) for i in range(RING_P)]
        maxs = sb("maxs", [P, 2, QT, 2, 4, NCH])
        negm = sb("negm", [P, 2, QT, 8])
        mrow = sb("mrow", [8, 2, NQ], BF16)
        osb = [sb(f"osb{i}", [P, 512]) for i in range(2)]
        rden = sb("rden", [P, QT, H])
        onr = sb("onr", [P, QT, D])
        ont = sb("ont", [P, NQ])
        x1 = sb("x1", [P, QT, D])
        x1a = sb("x1a", [P, QT, D])
        x1b = sb("x1b", [P, QT, D])
        if has_ctx:
            cin = sb("cin", [P, KT, D])
            srct = sb("srct", [P, KEYS])
        if spec.ctx_ln:
            cstats, cagg = sb("cstats", [P, KT, 6]), sb("cagg", [P, KT, 2])
            cs_v, cs_y, cs_t = sb("cs_v", [P, KT]), sb("cs_y", [P, KT]), sb("cs_t", [P, KT])
        if mlp:
            w1, w2 = sb("w1", [P, MLP]), sb("w2", [P, MC, D])
            b1_half = sb("b1_half", [P, MC])
            b1, b2_rows = sb("b1", [P, MC]), sb("b2_rows", [P, D])
            dcols, dgate = sb("dcols", [P, NC]), sb("dgate", [P, D])
            st2, ag2 = sb("st2", [P, QT, 6]), sb("ag2", [P, QT, 2])
            r2_v, r2_y, r2_t = sb("r2_v", [P, QT]), sb("r2_y", [P, QT]), sb("r2_t", [P, QT])
            xn2, x2t = sb("xn2", [P, QT, D]), sb("x2t", [P, NQ])
            z, hg, hu = sb("z", [P, MC, NQ]), sb("hg", [P, MC, NQ]), sb("hu", [P, MC, NQ])
            x2, x2a, x2b = sb("x2", [P, QT, D]), sb("x2a", [P, QT, D]), sb("x2b", [P, QT, D])

        sbank = [bank(f"scores{i}") for i in range(RING_S)]
        mbank = [bank(f"maxima{i}") for i in range(2)]
        obank, abank, dbank = bank("out"), bank("prep"), bank("post")

        consts = sem("consts")
        n_consts = 0
        ones_set = sem("ones_set")
        x_in, c_in = sem("x_in"), sem("c_in")
        x_ln = sem("x_ln")
        ln_dve = sem("ln_dve")
        c_ln, cln_dve = sem("c_ln"), sem("cln_dve")
        a_full, a_free = sem("prep_full"), sem("prep_free")
        q_r, q_split = sem("q_r"), sem("q_split")
        k_m, k_r, k_split = sem("k_m"), sem("k_r"), sem("k_split")
        q_out, k_out, q_st, k_st = sem("q_out"), sem("k_out"), sem("q_st"), sem("k_st")
        s_full, p_ready, pv_done = sem("scores_full"), sem("probs_ready"), sem("pv_done")
        m_full, m_free, m_neg = sem("maxima_full"), sem("maxima_free"), sem("neg_max")
        m_hi = sem("max_hi")
        m_out, m_st = sem("max_out"), sem("max_stacked")
        o_sb = sem("o_sb")
        d_full, d_free = sem("post_full"), sem("post_free")
        d_den, x_res, d_lin, d_x1 = sem("d_den"), sem("x_res"), sem("d_lin"), sem("d_x1")
        ln2, ln2_dve, x_out = sem("ln2"), sem("ln2_dve"), sem("x_out")
        g_p, g_e, g_h, d_fc2, d_x2 = (sem(n) for n in ("g_p", "g_e", "g_h", "d_fc2", "d_x2"))
        block = ctx.enter_context(nc.Block())

        A_AT = {k: i for i, k in enumerate(a_order)}
        D_AT = {k: i for i, k in enumerate(d_order)}
        X_IN = 16 * (2 if spec.q_cols or spec.k_cols else 1)
        LN_PER = 2 * QT + RSQRT_LINKS
        CLN_PER = 2 * KT + RSQRT_LINKS
        RES_PER = 16 * (1 + (1 if spec.gate is not None else 0) + (2 if mlp else 0))
        Q_ST_PER = 16 * 2 * 4
        K_ST_PER = 16 * 2 * 3
        LINX = 2 if spec.gate is not None else 1

        def walk(eng, step_c, step_m, step_r, step_a, step_d):
            def prologue():
                for st in SCHED:
                    if st[0] == "A":
                        step_a(st[1], 0, 0)
                for st in SCHED:
                    if st[0] == "M" and st[1] == 1:
                        step_m(st[2], st[3], st[4], st[5], 0, 0)
                    if st[0] == "R" and st[1] == 1:
                        step_r(st[2], 0, 0)

            def body(b, w, has_next, has_prev):
                for st in SCHED:
                    if st[0] == "C":
                        step_c(st[1], st[2], b, w)
                    elif st[0] == "M" and st[1] == 0:
                        step_m(st[2], st[3], st[4], st[5], b, w)
                    elif st[0] == "M" and has_next:
                        step_m(st[2], st[3], st[4], st[5], b + 1, 1 - w)
                    elif st[0] == "R" and st[1] == 0:
                        step_r(st[2], b, w)
                    elif st[0] == "R" and has_next:
                        step_r(st[2], b + 1, 1 - w)
                    elif st[0] == "A" and has_next:
                        step_a(st[1], b + 1, 1 - w)
                    elif st[0] == "D" and has_prev:
                        step_d(st[1], b - 1, 1 - w)

            def epilogue():
                for st in SCHED:
                    if st[0] == "D":
                        step_d(st[1], nb - 1, (nb - 1) % 2)

            prologue()
            body(0, 0, True, False)
            if nb > 2:
                with eng.Fori(0, (nb - 2) // 2) as i:
                    body(i * 2 + 1, 1, True, True)
                    body(i * 2 + 2, 0, True, True)
            body(nb - 1, 1, False, True)
            epilogue()

        def m_index(p, a, qt, ch):
            return p * UP + (a * QT + qt) * NCH + ch + (1 if p >= 5 else 0)

        R_INDEX = (5 * UP, PAIRS * UP + 1)

        def before(j, ring, per):
            if j >= ring:
                return j - ring
            last = max(k for k in range(per) if k % ring == j % ring)
            return last - per

        N_CONSTS = 5 + 2 * 16 + 2 + (4 if mlp else 0)
        N_SET = 11

        @block.sync
        def _(sp):
            nonlocal_consts = []

            def const(dst, src, slow=False):
                sp.dma_start(dst, src, allow_slow_non_contiguous=slow).then_inc(consts, 16)
                nonlocal_consts.append(1)

            def col(v):
                return v.rearrange("(c p) -> p c", p=P)

            def rows(v):
                return v.rearrange("(o n) -> o n", o=1).to_broadcast([P, D])

            const(ident[:], ident_d)
            for dst, src in ((wq, spec.wq), (wk, spec.wk), (wv, spec.wv), (wo, spec.wo)):
                const(dst[:], src)
            for dst, src in ((bq, spec.bq), (bk, spec.bk)):
                for par in range(2):
                    for d in range(HD):
                        at = par * 64 + d * PAIRS
                        const(dst[at:at + PAIRS, :], src.rearrange("(pair r one) -> r pair one", r=2 * HD, one=1)[par * HD + d], slow=True)
            const(bv[:], col(spec.bv), slow=True)
            const(bo_rows[:], rows(spec.bo))
            if mlp:
                const(w1[:], mlp["w1"])
                const(w2[:], mlp["w2"].rearrange("(c p) n -> p c n", p=P))
                const(b1[:], col(mlp["b1"]), slow=True)
                const(b2_rows[:], rows(mlp["b2"]))
            assert len(nonlocal_consts) == N_CONSTS

            def load_tokens(n, w):
                wait(sp, x_ln, n * QT)
                sp.dma_start(xin[:], spec.x_src[n].rearrange("(t p) d -> p t d", p=P)).then_inc(x_in, 16)
                if spec.q_cols or spec.k_cols:
                    wait(sp, a_free, after(n - 1, A_USES, A_AT["xt"]) if has_before(n) else 0)
                    sp.dma_start(acols[:], cols_d[n]).then_inc(x_in, 16)

            def load_ctx(n, w):
                if has_ctx:
                    wait(sp, a_full, after(n - 1, A_USES, A_AT["ctx3"]) if has_before(n) else 0)
                    src = spec.ctx[n]
                    sp.dma_start(cin[:, 0:KT - 1, :], src[0:(KT - 1) * P, :].rearrange("(t p) d -> p t d", p=P)).then_inc(c_in, 16)
                    sp.dma_start(cin[0:LAST, KT - 1, :], src[(KT - 1) * P:KEYS, :]).then_inc(c_in, 16)

            def stacks(n, w, first):
                wait(sp, k_split, after(n, 1, 0))
                sp.dma_start(k_scr[w].rearrange("s par d pair c -> (par d pair) s c"), ksp[:]).then_inc(k_out, 16)
                wait(sp, q_split, after(n, 2, 1))
                sp.dma_start(q_scr[w].rearrange("s par d pair c -> (par d pair) s c"), qsp[:]).then_inc(q_out, 16)
                if not first:
                    wait_apart(sp, s_full, after(n - 2, JC, JC - 1), (ones_set, N_SET))
                sp.wait_ge(k_out, after(n, 1, 0) * 16)
                for par in range(2):
                    for t, reps in ((0, 3), (3, 2), (5, 1)):
                        src = k_scr[w][K_PART[t], par].rearrange("d pair c -> d (pair c)")
                        if reps > 1:
                            src = src.unsqueeze(0).to_broadcast([reps, HD, PAIRS * KEYS])
                        at = par * ROWS + t * HD
                        sp.dma_start(kst[w][at:at + reps * HD].rearrange("p a c -> p (a c)"), src).then_inc(k_st, 16)
                sp.wait_ge(q_out, after(n, 1, 0) * 16)
                for par in range(2):
                    for t, parts in ((0, 3), (3, 2), (5, 1)):
                        at = par * ROWS + t * HD
                        src = q_scr[w][Q_PART[t]:Q_PART[t] + parts, par].rearrange("s d pair c -> s d (pair c)")
                        sp.dma_start(qst[w][at:at + parts * HD, par].rearrange("p a c -> p (a c)"), src).then_inc(q_st, 16)
                    at = par * ROWS + MAX_ROW
                    sp.dma_start(qst[w][at:at + 2, par].rearrange("p a c -> p (a c)"), zeros[:]).then_inc(q_st, 16)

            def max_rows(n, w, half):
                wait(sp, m_free, after(n, UM, R_INDEX[half]))
                sp.dma_start(m_scr[w, half].rearrange("par pair s c -> (par pair) s c"), mrow[:]).then_inc(m_out, 16)
                sp.wait_ge(m_out, after(n, 2, half) * 16)
                for par in range(2):
                    at = par * ROWS + MAX_ROW
                    sp.dma_start(qst[w][at:at + 2, par, 4 * half:4 * half + 4, :],
                                 m_scr[w, half, par].rearrange("pair s c -> s pair c")).then_inc(m_st, 16)

            def load_res(d):
                wait(sp, d_x1, d)
                if mlp:
                    wait(sp, d_x2, d)
                sp.dma_start(xres[:], spec.x_src[d].rearrange("(t p) d -> p t d", p=P)).then_inc(x_res, 16)
                if gate is not None:
                    sp.dma_start(gate[:], rows_d[d][spec.gate:spec.gate + 1, :].to_broadcast([P, D])).then_inc(x_res, 16)
                if mlp:
                    sp.dma_start(dcols[:], cols_d[d]).then_inc(x_res, 16)
                    sp.dma_start(dgate[:], rows_d[d][mlp["gate"]:mlp["gate"] + 1, :].to_broadcast([P, D])).then_inc(x_res, 16)

            def store(d):
                wait(sp, d_x2 if mlp else d_x1, after(d, 1, 0))
                sp.dma_start(spec.x_dst[d].rearrange("(t p) d -> p t d", p=P), (x2 if mlp else x1)[:]).then_inc(x_out, 16)

            def prologue():
                load_tokens(0, 0)
                load_ctx(0, 0)
                sp.wait_ge(ones_set, N_SET)
                stacks(0, 0, True)
                load_tokens(1, 1)
                load_ctx(1, 1)
                max_rows(0, 0, 0)

            def body(b, w, has_next, has_prev):
                if has_prev:
                    load_res(b - 1)
                if has_next:
                    stacks(b + 1, 1 - w, isinstance(b, int) and b == 0)
                max_rows(b, w, 1)
                if has_next and not (isinstance(b, int) and b == nb - 2):
                    load_tokens_guarded(b, w)
                if has_prev:
                    pass
                if has_next:
                    max_rows(b + 1, 1 - w, 0)
                if has_prev:
                    store(b - 1)

            def load_tokens_guarded(b, w):
                load_tokens(b + 2, w)
                load_ctx(b + 2, w)

            def epilogue():
                load_res(nb - 1)
                store(nb - 1)
                sp.wait_ge(x_out, 16 * nb)

            prologue()
            body(0, 0, True, False)
            if nb > 4:
                with sp.Fori(0, (nb - 4) // 2) as i:
                    body(i * 2 + 1, 1, True, True)
                    body(i * 2 + 2, 0, True, True)
            if nb > 2:
                body(nb - 3, 1, True, True)
                body(nb - 2, 0, True, True)
            body(nb - 1, 1, False, True)
            epilogue()


        @block.vector
        def _(dve):
            dve.memset(zeros[:], 0.0).then_inc(ones_set, 1)
            for i in range(2):
                dve.memset(vaug[i][:], 1.0).then_inc(ones_set, 1)
                dve.memset(qst[i][:], 0.0).then_inc(ones_set, 1)
                dve.memset(kst[i][:], 1.0).then_inc(ones_set, 1)
            dve.memset(obank[:], 0.0).then_inc(ones_set, 1)
            dve.wait_ge(consts, 16 * N_CONSTS)
            for dst, src in ((wqp, wq), (wkp, wk)):
                for par in range(2):
                    ins = dve.tensor_copy(dst[:, par * 64:(par + 1) * 64].rearrange("p (d pair) -> p d pair", pair=PAIRS),
                                          src[:].rearrange("p (pair par d) -> p par d pair", par=2, d=HD)[:, par])
                ins.then_inc(ones_set, 1)
            if spec.ctx_ln:
                dve.memset(cagg[:], 0.0)
            if mlp:
                dve.tensor_scalar(b1_half[:], b1[:], 0.5, None, ALU.mult)
            dve.memset(negm[:], 0.0).then_inc(ones_set, 1)
            dve.wait_ge(ones_set, N_SET)

            def step_c(q, t, b, w):
                halves = ([0] if (q, t) == (2, 0) else []) + ([1] if (q, t) == (QUADS - 1, KT - 1) else [])
                for half in halves:
                    wait(dve, pv_done, after(b, QUADS * KT, (half + 1) * 2 * KT - 1))
                    if has_before(b):
                        wait(dve, d_full, after(b - 1, D_USES, D_AT["o1"]))
                    dve.tensor_copy(osb[half][:], obank[:]).then_inc(o_sb, 1)

            def step_m(p, a, qt, ch, b, w):
                u = m_index(p, a, qt, ch)
                if p % 4 == 0 and a == qt == ch == 0:
                    wait(dve, m_neg, after(b - 1, 2, p // 4) if has_before(b) else 0)
                wait(dve, m_full, after(b, UM, u))
                width = CH[ch][1]
                dve.tensor_reduce(maxs[:, p // 4, qt, a, p % 4, ch:ch + 1], mbank[u % 2][:, 0:width], AX.X, ALU.max).then_inc(m_free, 1)

            def step_r(half, b, w):
                last = m_index(3 if half == 0 else 7, 1, QT - 1, NCH - 1)
                wait(dve, m_free, after(b, UM, last))
                if half or has_before(b):
                    wait(dve, m_full, after(b, UM, R_INDEX[0]) if half else after(b - 1, UM, R_INDEX[1]))
                dve.tensor_reduce(negm[:, half].rearrange("p t h -> p (t h)"), maxs[:, half].rearrange("p t a b c -> p (t a b) c"), AX.X, ALU.max,
                                  negate=True).then_inc(m_neg, 1)
                u = R_INDEX[half]
                wait(dve, m_full, after(b, UM, u))
                if half or has_before(b):
                    wait(dve, m_out, (after(b, 2, 0) if half else after(b - 1, 2, 1)) * 16)
                src = mbank[u % 2][0:8, 0:NQ]
                dve.tensor_copy(mrow[:, 0, :], src).then_inc(m_hi, 1)
                wait(dve, m_hi, after(b, 2, half))
                dve.tensor_tensor(mrow[:, 1, :], src, mrow[:, 0, :], ALU.subtract).then_inc(m_free, 1)

            def moments(chain_sem, per, b, src, st, ag, tiles):
                link = Chain(dve, chain_sem, b * per)
                for i, rows in enumerate(tiles):
                    link(dve.bn_stats(st[0:rows, i, :], src[0:rows, i, :]))
                link.join_apart((ones_set, N_SET))
                for i, rows in enumerate(tiles):
                    link(dve.bn_aggr(ag[0:rows, i, :], st[0:rows, i, :]))
                link.join()
                return link

            def step_a(k, n, w):
                if k == "ln":
                    wait(dve, x_in, after(n, 1, 0) * X_IN)
                    if has_before(n):
                        wait(dve, x_ln, n * QT)
                    link = moments(ln_dve, LN_PER, n, xin, stats, agg, [P] * QT)
                    rsqrt(dve, link, agg[:, :, 1], rs_v[:], rs_y[:], rs_t[:], spec.eps)
                    if has_before(n):
                        wait(dve, a_full, after(n - 1, A_USES, A_AT["xt"]))
                    for t in range(QT):
                        ins = dve.tensor_scalar(xn[:, t, :], xin[:, t, :], agg[:, t, 0:1], rs_y[:, t:t + 1], ALU.subtract, ALU.mult)
                        ins.then_inc(x_ln, 1)
                    if spec.ctx_ln:
                        wait(dve, c_in, (n + 1) * 32)
                        if has_before(n):
                            wait(dve, c_ln, n * KT)
                        tiles = [P] * (KT - 1) + [LAST]
                        link = moments(cln_dve, CLN_PER, n, cin, cstats, cagg, tiles)
                        rsqrt(dve, link, cagg[:, :, 1], cs_v[:], cs_y[:], cs_t[:], spec.ctx_ln)
                elif k[0] == "v":
                    g = int(k[1:])
                    wait(dve, a_full, after(n, A_USES, A_AT[k]))
                    if g == 0 and not (isinstance(n, int) and n < 2):
                        wait(dve, pv_done, after(n - 2, QUADS * KT, QUADS * KT - 1))
                    t0, cnt = TG[g]
                    full = cnt if t0 + cnt < KT else cnt - 1
                    src = abank[:].rearrange("p (t h d) -> p t h d", t=4, d=HD)
                    if full:
                        ins = dve.tensor_copy(vaug[w][:, t0:t0 + full, :, 0:HD], src[:, 0:full])
                    if full < cnt:
                        ins2 = dve.tensor_copy(vaug[w][0:LAST, KT - 1, :, 0:HD], src[0:LAST, full])
                        ins = ins2
                    ins.then_inc(a_free, 1)

            def step_d(k, d, w):
                if k in ("o0", "o1"):
                    qt = int(k[1])
                    wait(dve, d_full, after(d, D_USES, D_AT[k]))
                    src = dbank[:].rearrange("p (h r) -> p h r", r=32)
                    dve.reciprocal(rden[:, qt, :], src[:, :, HD]).then_inc(d_den, 1)
                    wait(dve, d_den, after(d, QT, qt))
                    dve.tensor_tensor(onr[:, qt, :].rearrange("p (h e) -> p h e", e=HD), src[:, :, 0:HD],
                                      rden[:, qt, :].unsqueeze(2).to_broadcast([P, H, HD]), ALU.mult).then_inc(d_free, 1)
                elif k == "proj":
                    wait(dve, d_full, after(d, D_USES, D_AT[k]))
                    if has_before(d):
                        wait(dve, d_x1, d)
                    dve.tensor_tensor(x1a[:], dbank[:, 0:QT * D].rearrange("p (t d) -> p t d", d=D),
                                      bo_rows[:].unsqueeze(1).to_broadcast([P, QT, D]), ALU.add).then_inc(d_free, 1)
                elif k == "x2t":
                    wait(dve, d_x1, after(d, 1, 0))
                    wait(dve, ln2, d * QT)
                    link = moments(ln2_dve, LN_PER, d, x1, st2, ag2, [P] * QT)
                    rsqrt(dve, link, ag2[:, :, 1], r2_v[:], r2_y[:], r2_t[:], mlp["eps"])
                    for t in range(QT):
                        dve.tensor_scalar(xn2[:, t, :], x1[:, t, :], ag2[:, t, 0:1], r2_y[:, t:t + 1], ALU.subtract, ALU.mult).then_inc(ln2, 1)
                elif k == "fc2":
                    wait(dve, g_e, after(d, 1, 0))
                    dve.scalar_tensor_tensor(out=hg[:].rearrange("p c n -> p (c n)"), in0=hu[:].rearrange("p c n -> p (c n)"), scalar=1.0,
                                             in1=z[:].rearrange("p c n -> p (c n)"), op0=ALU.add, op1=ALU.mult).then_inc(g_h, 1)
                    wait(dve, d_full, after(d, D_USES, D_AT[k]))
                    if has_before(d):
                        wait(dve, d_x2, d)
                    dve.tensor_tensor(x2a[:], dbank[:, 0:QT * D].rearrange("p (t d) -> p t d", d=D),
                                      b2_rows[:].unsqueeze(1).to_broadcast([P, QT, D]), ALU.add).then_inc(d_free, 1)

            walk(dve, step_c, step_m, step_r, step_a, step_d)

        @block.scalar
        def _(act):
            act.wait_ge(consts, 16 * N_CONSTS)
            act.wait_ge(ones_set, N_SET)

            def step_c(q, t, b, w):
                rows = LAST if t == KT - 1 else P
                for pp in range(2):
                    j = (q * KT + t) * 2 + pp
                    wait(act, s_full, after(b, JC, j))
                    if pp == 0:
                        i = before(q * KT + t, RING_P // 2, QUADS * KT)
                        wait(act, pv_done, after(b, QUADS * KT, i))
                    act.activation(probs[j % RING_P][0:rows, :], sbank[j % RING_S][0:rows, :], ACT.Exp,
                                   scale=HD ** -0.5).then_inc(p_ready, 1)

            def step_m(*_):
                pass

            def step_r(*_):
                pass

            def step_a(k, n, w):
                first = not has_before(n)
                if k[:3] == "ctx":
                    g = int(k[3:])
                    wait(act, a_full, after(n, A_USES, A_AT[k]))
                    if g == 0 and not first:
                        wait(act, a_full, after(n - 1, A_USES, A_AT["v3"]))
                    t0, cnt = TG[g]
                    width = min(KEYS, (t0 + cnt) * P) - t0 * P
                    dst, src = srct[:, t0 * P:t0 * P + width], abank[:, 0:width]
                    if spec.k_cols:
                        wait(act, x_in, after(n, 1, 0) * X_IN)
                        act.activation(dst, src, ACT.Identity, bias=column(acols, spec.k_cols[1]), scale=column(acols, spec.k_cols[0])).then_inc(a_free, 1)
                    else:
                        act.activation(dst, src, ACT.Identity).then_inc(a_free, 1)
                elif k == "xt":
                    wait(act, a_full, after(n, A_USES, A_AT[k]))
                    if not first:
                        wait(act, a_full, after(n - 1, A_USES, A_AT["v0" if not has_ctx else "q"]))
                    if spec.q_cols:
                        wait(act, x_in, after(n, 1, 0) * X_IN)
                        act.activation(xmt[:], abank[:, 0:NQ], ACT.Identity, bias=column(acols, spec.q_cols[1]), scale=column(acols, spec.q_cols[0])).then_inc(a_free, 1)
                    else:
                        act.activation(xmt[:], abank[:, 0:NQ], ACT.Identity).then_inc(a_free, 1)
                elif k == "q":
                    wait(act, a_full, after(n, A_USES, A_AT[k]))
                    if not first:
                        wait(act, q_out, n * 16)
                    act.activation(qf[:], abank[:, 0:NQ], ACT.Identity, bias=bq[:])
                    act.activation(qsp[:, 0, :], abank[:, 0:NQ], ACT.Identity, bias=bq[:]).then_inc(a_free, 1)
                elif k[0] == "k" and k[1:].isdigit():
                    c = int(k[1:])
                    at, width = CH[c]
                    wait(act, a_full, after(n, A_USES, A_AT[k]))
                    if c == 0 and not first:
                        wait(act, k_out, n * 16)
                    act.activation(kf[:, at:at + width], abank[:, 0:width], ACT.Identity, bias=bk[:])
                    act.activation(ksp[:, 0, at:at + width], abank[:, 0:width], ACT.Identity, bias=bk[:]).then_inc(a_free, 1)
                elif k == "ksplit":
                    for c, (at, width) in enumerate(CH):
                        wait(act, k_r, after(n, NCH, c))
                        act.activation(ksp[:, 1, at:at + width], kr[:, at:at + width], ACT.Identity).then_inc(k_m, 1)

            def step_d(k, d, w):
                first = not has_before(d)
                if k == "ot":
                    wait(act, d_full, after(d, D_USES, D_AT[k]))
                    act.activation(ont[:], dbank[:, 0:NQ], ACT.Identity, bias=bv[:]).then_inc(d_free, 1)
                elif k == "x2t":
                    wait(act, d_full, after(d, D_USES, D_AT[k]))
                    wait(act, x_res, after(d, 1, 0) * RES_PER)
                    act.activation(x2t[:], dbank[:, 0:NQ], ACT.Identity, bias=column(dcols, mlp["cols"][1]), scale=column(dcols, mlp["cols"][0])).then_inc(d_free, 1)
                elif k in ("h0", "h1"):
                    half = int(k[1])
                    wait(act, d_full, after(d, D_USES, D_AT[k]))
                    if not first:
                        wait(act, g_h, d)
                    for c in range(2):
                        cc = 2 * half + c
                        ins = act.activation(z[:, cc, :], dbank[:, c * NQ:(c + 1) * NQ], ACT.Identity, bias=b1_half[:, cc:cc + 1], scale=0.5)
                    ins.then_inc(d_free, 1)
                    if half == 1:
                        wait(act, g_p, after(d, 3, 2))
                        act.activation(hu[:], hg[:], ACT.Tanh, scale=2.0 * GELU_SCALE).then_inc(g_e, 1)

            walk(act, step_c, step_m, step_r, step_a, step_d)

        @block.gpsimd
        def _(pool):
            def step_a(k, n, w):
                first = not has_before(n)
                if k == "ln" and spec.ctx_ln:
                    wait_apart(pool, cln_dve, (n + 1) * CLN_PER, (ones_set, N_SET))
                    for t in range(KT):
                        rows = LAST if t == KT - 1 else P
                        pool.tensor_scalar(cin[0:rows, t, :], cin[0:rows, t, :], cagg[0:rows, t, 0:1], cs_y[0:rows, t:t + 1],
                                           ALU.subtract, ALU.mult).then_inc(c_ln, 1)
                elif k[0] == "k" and k[1:].isdigit():
                    c = int(k[1:])
                    part = slice(CH[c][0], CH[c][0] + CH[c][1])
                    wait(pool, a_free, after(n, A_USES, A_AT[k]))
                    if c == 0:
                        wait(pool, k_split, n)
                    pool.tensor_tensor(kr[:, part], kf[:, part], ksp[:, 0, part], ALU.subtract).then_inc(k_r, 1)
                elif k == "ksplit":
                    wait(pool, k_m, (n + 1) * NCH)
                    pool.tensor_tensor(ksp[:, 2, :], kr[:], ksp[:, 1, :], ALU.subtract).then_inc(k_split, 1)
                elif k == "q":
                    wait(pool, a_free, after(n, A_USES, A_AT[k]))
                    if not first:
                        wait(pool, q_split, n * 2)
                    pool.tensor_tensor(qr[:], qf[:], qsp[:, 0, :], ALU.subtract).then_inc(q_r, 1)
                    wait_apart(pool, q_r, after(n, 1, 0), (ones_set, N_SET))
                    pool.tensor_copy(qsp[:, 1, :], qr[:]).then_inc(q_split, 1)
                    wait(pool, q_split, n * 2 + 1)
                    pool.tensor_tensor(qsp[:, 2, :], qr[:], qsp[:, 1, :], ALU.subtract).then_inc(q_split, 1)

            def step_d(k, d, w):
                first = not has_before(d)
                if k == "proj":
                    wait(pool, d_free, after(d, D_USES, D_AT[k]))
                    wait(pool, x_res, after(d, 1, 0) * RES_PER)
                    src = x1a
                    wait(pool, d_x1, d)
                    if gate is not None:
                        pool.tensor_tensor(x1b[:], x1a[:], gate[:].unsqueeze(1).to_broadcast([P, QT, D]), ALU.mult).then_inc(d_lin, 1)
                        pool.wait_ge(d_lin, after(d, 1, 0))
                        src = x1b
                    if not first:
                        wait(pool, d_x2 if mlp else x_out, d if mlp else d * 16)
                    pool.tensor_tensor(x1[:], src[:], xres[:], ALU.add).then_inc(d_x1, 1)
                elif k == "h1":
                    wait(pool, d_free, after(d, D_USES, D_AT[k]))
                    if not first:
                        wait(pool, g_h, d)
                    pool.tensor_tensor(hg[:], z[:], z[:], ALU.mult).then_inc(g_p, 1)
                    wait_apart(pool, g_p, after(d, 3, 0), (ones_set, N_SET))
                    pool.tensor_scalar(hu[:], hg[:], 4 * GELU_CUBE, 1.0, ALU.mult, ALU.add).then_inc(g_p, 1)
                    pool.wait_ge(g_p, after(d, 3, 1))
                    pool.tensor_tensor(hg[:], hu[:], z[:], ALU.mult).then_inc(g_p, 1)
                elif k == "fc2":
                    wait(pool, d_free, after(d, D_USES, D_AT[k]))
                    wait(pool, d_x2, d)
                    pool.tensor_tensor(x2b[:], x2a[:], dgate[:].unsqueeze(1).to_broadcast([P, QT, D]), ALU.mult).then_inc(d_fc2, 1)
                    pool.wait_ge(d_fc2, after(d, 1, 0))
                    if not first:
                        wait(pool, x_out, d * 16)
                    pool.tensor_tensor(x2[:], x2b[:], x1[:], ALU.add).then_inc(d_x2, 1)

            walk(pool, lambda *_: None, lambda *_: None, lambda *_: None, step_a, step_d)

        @block.tensor
        def _(pe):
            pe.wait_ge(consts, 16 * N_CONSTS)
            pe.wait_ge(ones_set, N_SET)
            steps = QUADS * KT

            def scores(q, t, b, w):
                rows = LAST if t == KT - 1 else P
                if t == 0 and q % 2 == 0:
                    wait(pe, m_st, after(b, 2, q // 2) * 32)
                for pp in range(2):
                    j = (q * KT + t) * 2 + pp
                    pair = 2 * q + pp
                    wait(pe, p_ready, after(b, JC, before(j, RING_S, JC)))
                    pe.matmul(sbank[j % RING_S][0:rows, :], kst[w][:, pair, t * P:t * P + rows],
                              qst[w][:, :, pair, :], start=True, stop=True).then_inc(s_full, 1)

            def values(q, t, b, w):
                rows = LAST if t == KT - 1 else P
                j = (q * KT + t) * 2
                wait(pe, p_ready, after(b, JC, j + 1))
                if t == 0 and q % 2 == 0:
                    wait(pe, o_sb, after(b, 2, q // 2 - 1))
                for h4 in range(4):
                    ins = pe.matmul(obank[32 * h4:32 * h4 + HD + 1, (q % 2) * NQ:(q % 2 + 1) * NQ],
                                    vaug[w][0:rows, t, 4 * q + h4, :],
                                    probs[(j + h4 // 2) % RING_P][0:rows, (h4 % 2) * NQ:(h4 % 2 + 1) * NQ],
                                    start=(t == 0), stop=(t == KT - 1))
                ins.then_inc(pv_done, 1)

            def step_c(q, t, b, w):
                scores(q, t, b, w)
                i = q * KT + t
                if i > 0:
                    values((i - 1) // KT, (i - 1) % KT, b, w)
                if i == steps - 1:
                    values(q, t, b, w)

            def step_m(p, a, qt, ch, b, w):
                u = m_index(p, a, qt, ch)
                if u == 0:
                    wait(pe, q_st, after(b, 1, 0) * Q_ST_PER)
                    wait(pe, k_st, after(b, 1, 0) * K_ST_PER)
                wait(pe, m_free, after(b, UM, before(u, 2, UM)))
                at, width = CH[ch]
                pe.matmul(mbank[u % 2][:, 0:width], qst[w][:, a, p, qt * P:(qt + 1) * P], kst[w][:, p, at:at + width],
                          start=True, stop=True).then_inc(m_full, 1)

            def step_r(half, b, w):
                u = R_INDEX[half]
                wait(pe, m_neg, after(b, 2, half))
                wait(pe, m_free, after(b, UM, before(u, 2, UM)))
                for qt in range(QT):
                    ins = pe.transpose(mbank[u % 2][0:8, qt * P:(qt + 1) * P], negm[:, half, qt, :], ident[:])
                ins.then_inc(m_full, 1)

            def step_a(k, n, w):
                if k in ("ln", "ksplit"):
                    return
                wait(pe, a_free, after(n, A_USES, A_AT[k] - 1))
                if k[:3] == "ctx":
                    t0, cnt = TG[int(k[3:])]
                    if not spec.ctx_ln:
                        wait(pe, c_in, (n + 1) * 32)
                    for t in range(t0, t0 + cnt):
                        rows = LAST if t == KT - 1 else P
                        if spec.ctx_ln:
                            wait(pe, c_ln, after(n, KT, t))
                        ins = pe.transpose(abank[:, (t - t0) * P:(t - t0) * P + rows], cin[0:rows, t, :], ident[0:rows, 0:rows])
                elif k == "xt":
                    wait(pe, x_ln, (n + 1) * QT)
                    for t in range(QT):
                        ins = pe.transpose(abank[:, t * P:(t + 1) * P], xn[:, t, :], ident[:])
                elif k == "q":
                    ins = pe.matmul(abank[:, 0:NQ], wqp[:], xmt[:], start=True, stop=True)
                elif k[0] == "k":
                    at, width = CH[int(k[1:])]
                    src = srct[:, at:at + width] if has_ctx else xmt[:]
                    ins = pe.matmul(abank[:, 0:width], wkp[:], src, start=True, stop=True)
                else:
                    t0, cnt = TG[int(k[1:])]
                    for t in range(t0, t0 + cnt):
                        rows = LAST if t == KT - 1 else P
                        src = (srct if has_ctx else xmt)[:, t * P:t * P + rows]
                        ins = pe.matmul(abank[0:rows, (t - t0) * P:(t - t0 + 1) * P], src, wv[:], start=True, stop=True)
                ins.then_inc(a_full, 1)

            def step_d(k, d, w):
                wait(pe, d_free, after(d, D_USES, D_AT[k] - 1))
                if k in ("o0", "o1"):
                    qt = int(k[1])
                    wait(pe, o_sb, (d + 1) * 2)
                    for g in range(QUADS):
                        at = (g % 2) * NQ + qt * P
                        ins = pe.transpose(dbank[:, g * P:(g + 1) * P], osb[g // 2][:, at:at + P], ident[:])
                elif k == "ot":
                    for t in range(QT):
                        ins = pe.transpose(dbank[:, t * P:(t + 1) * P], onr[:, t, :], ident[:])
                elif k == "proj":
                    for t in range(QT):
                        ins = pe.matmul(dbank[:, t * D:(t + 1) * D], ont[:, t * P:(t + 1) * P], wo[:], start=True, stop=True)
                elif k == "x2t":
                    wait(pe, ln2, (d + 1) * QT)
                    for t in range(QT):
                        ins = pe.transpose(dbank[:, t * P:(t + 1) * P], xn2[:, t, :], ident[:])
                elif k in ("h0", "h1"):
                    for c in range(2):
                        cc = 2 * int(k[1]) + c
                        ins = pe.matmul(dbank[:, c * NQ:(c + 1) * NQ], w1[:, cc * P:(cc + 1) * P], x2t[:], start=True, stop=True)
                elif k == "fc2":
                    wait(pe, g_h, after(d, 1, 0))
                    for t in range(QT):
                        for c in range(MC):
                            ins = pe.matmul(dbank[:, t * D:(t + 1) * D], hg[:, c, t * P:(t + 1) * P], w2[:, c, :],
                                            start=(c == 0), stop=(c == MC - 1))
                ins.then_inc(d_full, 1)

            walk(pe, step_c, step_m, step_r, step_a, step_d)


N_COLS = 19
N_ROWS = 5
ROUTER_ROW = 4
EXPERTS = 3
RH = 256
L0_COLS, L2_COLS, L3_COLS, L1_COLS = 0, 4, 8, 12


def modulation(nc, w, cols_d, rows_d, ident_d):
    with Semaphores(nc) as sems, ExitStack() as ctx:
        def sb(name, shape, dt=F32):
            return ctx.enter_context(nc.sbuf_tensor(f"mod_{name}", shape, dt))

        def sem(name):
            return sems(f"mod_{name}")

        ident = sb("ident", [P, P])
        cond = sb("cond", [B, D])
        half, tanh_, silu = sb("half", [B, D]), sb("tanh", [B, D]), sb("silu", [B, D])
        silu_t, cond_t = sb("silu_t", [P, B]), sb("cond_t", [P, B])
        w0, w3 = sb("w0", [P, 6, D]), sb("w3", [P, 6, D])
        w2q, w2k = sb("w2q", [P, 2, D]), sb("w2k", [P, 2, D])
        b0, b3 = sb("b0", [P, 6]), sb("b3", [P, 6])
        b2q, b2k = sb("b2q", [P, 2]), sb("b2k", [P, 2])
        we, be = sb("we", [P, EXPERTS, 2, D]), sb("be", [P, EXPERTS * 2])
        wg, bg = sb("wg", [P, D]), sb("bg", [P, 1])
        wr = sb("wr", [P, EXPERTS])
        brow0, brow3, brow_r = sb("brow0", [1, 6, D]), sb("brow3", [1, 6, D]), sb("brow_r", [1, EXPERTS])
        ones = sb("ones", [1, B])
        cols, rows = sb("cols", [P, B, N_COLS]), sb("rows", [B, N_ROWS, D])
        tbank = ctx.enter_context(nc.psum_tensor("mod_t", [P, 512], F32))
        cbank = ctx.enter_context(nc.psum_tensor("mod_c", [P, 512], F32))
        rbank = [ctx.enter_context(nc.psum_tensor(f"mod_r{i}", [P, 512], F32)) for i in range(2)]
        loaded, ready, made, turned, products, moved, out = (sem(n) for n in (
            "loaded", "constants", "silu", "turned", "products", "moved", "out"))
        block = ctx.enter_context(nc.Block())
        loads = [(ident[:], ident_d, False), (cond[:], w["cond"], False),
                 (w0[:], w["w0"].rearrange("p (c n) -> p c n", n=D), False), (w3[:], w["w3"].rearrange("p (c n) -> p c n", n=D), False),
                 (w2q[:], w["w2q"].rearrange("p (c n) -> p c n", n=D), False), (w2k[:], w["w2k"].rearrange("p (c n) -> p c n", n=D), False),
                 (b0[:], w["b0"].rearrange("(c p) -> p c", p=P), True), (b3[:], w["b3"].rearrange("(c p) -> p c", p=P), True),
                 (b2q[:], w["b2q"].rearrange("(c p) -> p c", p=P), True), (b2k[:], w["b2k"].rearrange("(c p) -> p c", p=P), True),
                 (wg[:], w["gate_w1"][2 * D:3 * D, :], False), (bg[:], w["gate_b1"].rearrange("(c p) -> p c", p=P), True),
                 (wr[:], w["router_w"][2 * D:3 * D, :], False),
                 (brow0[:], w["b0"].rearrange("(o c n) -> o c n", o=1, n=D), False), (brow3[:], w["b3"].rearrange("(o c n) -> o c n", o=1, n=D), False),
                 (brow_r[:], w["router_b"].rearrange("(o n) -> o n", o=1), False)]
        for e in range(EXPERTS):
            loads.append((we[:, e], w["e_w1"][e, 2 * D:3 * D, :].rearrange("p (c n) -> p c n", n=D), False))
            loads.append((be[:, 2 * e:2 * e + 2], w["e_b1"][e].rearrange("(c p) -> p c", p=P), True))
        col_of = []
        for wt, bt in ((w0, b0), (w3, b3)):
            col_of.append([(wt[:, c], bt[:, c:c + 1], silu_t, ALU.add, add) for c, add in ((1, 1.0), (0, 0.0), (4, 1.0), (3, 0.0))])
        kv_cols = [(wt[:, c], bt[:, c:c + 1], silu_t, ALU.add, add) for wt, bt in ((w2q, b2q), (w2k, b2k)) for c, add in ((0, 1.0), (1, 0.0))]
        anchor = [(we[:, i // 2, i % 2], be[:, i:i + 1], cond_t, ALU.mult, 0.5) for i in range(2 * EXPERTS)] + [(wg[:], bg[:], cond_t, ALU.mult, 0.5)]
        columns = col_of[0] + kv_cols + col_of[1] + anchor
        assert len(columns) == N_COLS

        @block.sync
        def _(sp):
            for dst, src, slow in loads:
                sp.dma_start(dst, src, allow_slow_non_contiguous=slow).then_inc(loaded, 16)
            sp.wait_ge(moved, N_COLS + 3)
            sp.dma_start(cols_d.rearrange("b p c -> p b c"), cols[:]).then_inc(out, 16)
            sp.dma_start(rows_d, rows[:]).then_inc(out, 16)
            sp.wait_ge(out, 32)

        @block.scalar
        def _(act):
            act.wait_ge(loaded, 16 * len(loads))
            act.activation(half[:], cond[:], ACT.Copy, scale=0.5).then_inc(made, 1)
            act.wait_ge(made, 1)
            act.activation(tanh_[:], half[:], ACT.Tanh).then_inc(made, 1)

        @block.vector
        def _(dve):
            dve.memset(ones[:], 1.0).then_inc(ready, 1)
            dve.memset(rows[:], 0.0).then_inc(ready, 1)
            dve.wait_ge(made, 2)
            dve.scalar_tensor_tensor(out=silu[:], in0=tanh_[:], scalar=1.0, in1=half[:], op0=ALU.add, op1=ALU.mult).then_inc(made, 1)
            dve.wait_ge(turned, 1)
            dve.tensor_copy(silu_t[:], tbank[:, 0:B])
            dve.tensor_copy(cond_t[:], tbank[:, B:2 * B]).then_inc(turned, 1)
            dve.wait_ge(products, 1)
            for c, (_, bias, _, op, by) in enumerate(columns):
                dve.tensor_scalar(cols[:, :, c], cbank[:, c * B:(c + 1) * B], bias, by, ALU.add, op).then_inc(moved, 1)
            dve.wait_ge(products, 2)
            dve.wait_ge(ready, 2)
            for i in range(2):
                dve.tensor_copy(rows[:, 2 * i:2 * i + 2, :], rbank[i][0:B, 0:2 * D].rearrange("b (c n) -> b c n", n=D)).then_inc(moved, 1)
            dve.tensor_copy(rows[:, ROUTER_ROW, 0:EXPERTS], rbank[0][0:B, 2 * D:2 * D + EXPERTS]).then_inc(moved, 1)

        @block.tensor
        def _(pe):
            pe.wait_ge(loaded, 16 * len(loads))
            pe.wait_ge(ready, 1)
            pe.wait_ge(made, 3)
            pe.transpose(tbank[:, 0:B], silu[:], ident[0:B, 0:B])
            pe.transpose(tbank[:, B:2 * B], cond[:], ident[0:B, 0:B]).then_inc(turned, 1)
            pe.wait_ge(turned, 2)
            for c, (wt, _, src, _, _) in enumerate(columns):
                ins = pe.matmul(cbank[:, c * B:(c + 1) * B], wt, src[:], start=True, stop=True)
            ins.then_inc(products, 1)
            for i, (wt, bt) in enumerate(((w0, brow0), (w3, brow3))):
                for k, c in enumerate((2, 5)):
                    dst = rbank[i][0:B, k * D:(k + 1) * D]
                    pe.matmul(dst, silu_t[:], wt[:, c], start=True, stop=False)
                    pe.matmul(dst, ones[:], bt[0:1, c], start=False, stop=True)
            dst = rbank[0][0:B, 2 * D:2 * D + EXPERTS]
            pe.matmul(dst, cond_t[:], wr[:], start=True, stop=False)
            pe.matmul(dst, ones[:], brow_r[:], start=False, stop=True).then_inc(products, 1)


def expert_layer(nc, w, x_src, x_dst, ctx_d, cols_d, rows_d, ident_d, nb):
    KEYS, KT = S, -(-S // P)
    LAST = KEYS - (KT - 1) * P
    CH = chunks_of(KEYS, 512)
    NCH = len(CH)
    TG = [(g, min(4, KT - g)) for g in range(0, KT, 4)]
    EPS = 1e-5
    FRONT = ["xt", "q", "qk", "c0", "c1", "c2", "c3"] + [f"p{qt}{g}" for qt in range(QT) for g in range(len(TG))] + ["pc", "ev"]
    BACK = ["r", "h0", "h1", "h2", "g1", "e0", "e1", "g2", "rt", "o"]
    UF, UB = len(FRONT), len(BACK)
    F_AT = {k: i for i, k in enumerate(FRONT)}
    B_AT = {k: i for i, k in enumerate(BACK)}
    FRONT_ORDER = ["ln", "xt", "q", "qk", "c0", "c1", "c2", "c3", "s0", "s1"] + [k for k in FRONT if k[0] == "p" and k != "pc"] + ["pc", "ev"]
    marks = [((i + 0.5) / len(FRONT_ORDER), ("F", k)) for i, k in enumerate(FRONT_ORDER)]
    marks += [((i + 0.4) / len(BACK), ("B", k)) for i, k in enumerate(BACK)]
    SCHED = [st for _, st in sorted(marks)]

    with Semaphores(nc) as sems, ExitStack() as ctx:
        def sb(name, shape, dt=F32):
            return ctx.enter_context(nc.sbuf_tensor(f"moe_{name}", shape, dt))

        def sem(name):
            return sems(f"moe_{name}")

        def bank(name):
            return ctx.enter_context(nc.psum_tensor(f"moe_bank_{name}", [P, 512], F32))

        ident = sb("ident", [P, P])
        wq, wk, wkt, wv = (sb(n, [P, D]) for n in ("wq", "wk", "wkt", "wv"))
        gam, bet = sb("gam", [P, 1]), sb("bet", [P, 1])
        ew1, ew2 = sb("ew1", [P, EXPERTS, 2, RH]), sb("ew2", [P, EXPERTS, 2, D])
        gw1, gw2, ow = sb("gw1", [P, 2, D]), sb("gw2", [P, D]), sb("ow", [P, D])
        rw = sb("rw", [P, 2, EXPERTS])
        eb2, gb2, ob = sb("eb2", [1, EXPERTS, D]), sb("gb2", [1, D]), sb("ob", [1, D])
        ones = sb("ones", [1, P])
        xin = [sb(f"xin{i}", [P, QT, D]) for i in range(2)]
        cin = sb("cin", [P, KT, D])
        acols = [sb(f"acols{i}", [P, N_COLS]) for i in range(2)]
        rrow = [sb(f"rrow{i}", [P, EXPERTS]) for i in range(2)]
        st, ag = sb("st", [P, QT, 6]), sb("ag", [P, QT, 2])
        rs_v, rs_y, rs_t = sb("rs_v", [P, QT]), sb("rs_y", [P, QT]), sb("rs_t", [P, QT])
        xn = sb("xn", [P, QT, D])
        nxt = [sb(f"nxt{i}", [P, NQ]) for i in range(2)]
        evt = [sb(f"evt{i}", [P, NQ]) for i in range(2)]
        q, qk = sb("q", [P, NQ]), sb("qk", [P, NQ])
        ct = sb("ct", [P, KEYS])
        mx, nm = sb("mx", [P, QT, NCH]), sb("nm", [P, QT])
        pr = [sb(f"pr{i}", [P, KEYS]) for i in range(QT)]
        sums, tot, rec = sb("sums", [P, QT, NCH]), sb("tot", [P, QT]), sb("rec", [P, QT])
        prn = [sb(f"prn{i}", [P, KEYS]) for i in range(QT)]
        pt = sb("pt", [P, KT, QT, P])
        pct = sb("pct", [P, NQ])
        lg, lm, le, ls = sb("lg", [P, QT, EXPERTS]), sb("lm", [P, QT]), sb("le", [P, QT, EXPERTS]), sb("ls", [P, QT])
        lx, rp = sb("lx", [P, QT, EXPERTS]), sb("rp", [P, QT, EXPERTS])
        hz, ht = sb("hz", [P, 2, NQ]), sb("ht", [P, 2, NQ])
        hh = sb("hh", [P, EXPERTS, 2, NQ])
        gz, gt, g1 = sb("gz", [P, NQ]), sb("gt", [P, NQ]), sb("g1", [P, NQ])
        acc = [sb(f"acc{i}", [P, D]) for i in range(2)]
        rt, rtt = sb("rt", [P, QT, D]), sb("rtt", [P, NQ])
        g2t, g2 = sb("g2t", [P, QT, D]), sb("g2", [P, QT, D])
        y, xo = sb("y", [P, QT, D]), sb("xo", [P, QT, D])
        sbank = [bank(f"s{i}") for i in range(4)]
        fbank = [bank(f"f{i}") for i in range(2)]
        gbank = [bank(f"g{i}") for i in range(2)]
        consts, ready, wk_turned = sem("consts"), sem("ready"), sem("wk_turned")
        x_in, c_in = [sem("x_in0"), sem("x_in1")], sem("c_in")
        ln_dve, x_ln = sem("ln_dve"), sem("x_ln")
        f_full, f_free = sem("front_full"), [sem("front_free0"), sem("front_free1")]
        b_full, b_free = sem("back_full"), [sem("back_free0"), sem("back_free1")]
        s_full, s_max, s_neg, s_exp, s_sum, s_rec, s_norm = (sem(n) for n in ("s_full", "s_max", "s_neg", "s_exp", "s_sum", "s_rec", "s_norm"))
        r_dve, r_exp = sem("r_dve"), sem("r_exp")
        h_tanh, h_out, r_acc, g_out, x_sum, x_out = (sem(n) for n in ("h_tanh", "h_out", "r_acc", "g_out", "x_sum", "x_out"))
        block = ctx.enter_context(nc.Block())

        consts_list = [(ident[:], ident_d, False), (wq[:], w["wq"], False), (wk[:], w["wk"], False), (wv[:], w["wv"], False),
                       (gam[:], w["gamma"].rearrange("(c p) -> p c", p=P), True), (bet[:], w["beta"].rearrange("(c p) -> p c", p=P), True),
                       (gw1[:], w["gate_w1"][0:2 * D].rearrange("(c p) n -> p c n", p=P), False), (gw2[:], w["gate_w2"], False),
                       (ow[:], w["out_w"], False), (rw[:], w["router_w"][0:2 * D].rearrange("(c p) n -> p c n", p=P), False),
                       (eb2[:], w["e_b2"].rearrange("(o e) n -> o e n", o=1), False), (gb2[:], w["gate_b2"].rearrange("(o n) -> o n", o=1), False),
                       (ob[:], w["out_b"].rearrange("(o n) -> o n", o=1), False)]
        for e in range(EXPERTS):
            consts_list.append((ew1[:, e], w["e_w1"][e, 0:2 * D].rearrange("(c p) n -> p c n", p=P), False))
            consts_list.append((ew2[:, e], w["e_w2"][e].rearrange("(c p) n -> p c n", p=P), False))
        X_LOADS = 3 * 16
        LN_PER = 2 * QT + RSQRT_LINKS
        F_USES = [(UF + 1) // 2, UF // 2]
        B_USES = [(UB + 1) // 2, UB // 2]
        ACCS = EXPERTS - 1
        R_PER = 5

        def f_done(n, i):
            return f_free[i % 2], after(n, F_USES[i % 2], i // 2)

        def b_done(d, i):
            return b_free[i % 2], after(d, B_USES[i % 2], i // 2)

        def bank_free(eng, done, n, i, per):
            if i >= 2:
                sem_, value = done(n, i - 2)
            else:
                sem_, value = done(n - 1, max(k for k in range(per) if k % 2 == i % 2))
            wait(eng, sem_, value)

        def walk(eng, front, back):
            def body(b, w, has_next):
                for kind, k in SCHED:
                    if kind == "F" and has_next:
                        front(k, b + 1, 1 - w)
                    elif kind == "B":
                        back(k, b, w)

            for kind, k in SCHED:
                if kind == "F":
                    front(k, 0, 0)
            body(0, 0, True)
            if nb > 2:
                with eng.Fori(0, (nb - 2) // 2) as i:
                    body(i * 2 + 1, 1, True)
                    body(i * 2 + 2, 0, True)
            body(nb - 1, 1, False)

        def move_probs(eng, copy, k, n):
            qt, g = int(k[1]), int(k[2])
            i, (t0, cnt) = F_AT[k], TG[g]
            wait(eng, f_full, after(n, UF, i))
            wait(eng, f_full, after(n - 1, UF, F_AT["pc"]))
            full = cnt if t0 + cnt < KT else cnt - 1
            src = fbank[i % 2][:].rearrange("p (t q) -> p t q", q=P)
            if full:
                ins = copy(pt[:, t0:t0 + full, qt, :], src[:, 0:full])
            if full < cnt:
                ins = copy(pt[0:LAST, KT - 1, qt, :], src[0:LAST, full])
            ins.then_inc(f_done(n, i)[0], 1)

        @block.sync
        def _(sp):
            for dst, src, slow in consts_list:
                sp.dma_start(dst, src, allow_slow_non_contiguous=slow).then_inc(consts, 16)

            def load_x(n, w):
                wait(sp, x_sum, n - 1)
                sp.dma_start(xin[w][:], x_src[n].rearrange("(t p) d -> p t d", p=P)).then_inc(x_in[w], 16)
                sp.dma_start(acols[w][:], cols_d[n]).then_inc(x_in[w], 16)
                sp.dma_start(rrow[w][:], rows_d[n][ROUTER_ROW:ROUTER_ROW + 1, 0:EXPERTS].to_broadcast([P, EXPERTS])).then_inc(x_in[w], 16)

            def load_c(n):
                wait(sp, f_full, after(n - 1, UF, F_AT["pc"]))
                src = ctx_d[n]
                sp.dma_start(cin[:, 0:KT - 1, :], src[0:(KT - 1) * P, :].rearrange("(t p) d -> p t d", p=P)).then_inc(c_in, 16)
                sp.dma_start(cin[0:LAST, KT - 1, :], src[(KT - 1) * P:KEYS, :]).then_inc(c_in, 16)

            def store(d):
                wait(sp, x_sum, d + 1)
                sp.dma_start(x_dst[d].rearrange("(t p) d -> p t d", p=P), xo[:]).then_inc(x_out, 16)

            load_x(0, 0)
            load_c(0)
            load_x(1, 1)
            load_c(1)
            store(0)
            if nb > 2:
                with sp.Fori(0, (nb - 2) // 2) as i:
                    for k, w in ((2, 0), (3, 1)):
                        load_x(i * 2 + k, w)
                        load_c(i * 2 + k)
                        store(i * 2 + k - 1)
            store(nb - 1)
            sp.wait_ge(x_out, 16 * nb)

        @block.vector
        def _(dve):
            dve.memset(ones[:], 1.0).then_inc(ready, 1)
            dve.wait_ge(wk_turned, 1)
            dve.tensor_copy(wkt[:], gbank[0][:, 0:P]).then_inc(wk_turned, 1)

            def front(k, n, w):
                if k == "ln":
                    dve.wait_ge(x_in[w], (n - w) * (X_LOADS // 2) + X_LOADS)
                    wait(dve, x_ln, n * QT)
                    link = Chain(dve, ln_dve, n * LN_PER)
                    for t in range(QT):
                        link(dve.bn_stats(st[:, t, :], xin[w][:, t, :]))
                    link.join_apart((ready, 1))
                    for t in range(QT):
                        link(dve.bn_aggr(ag[:, t, :], st[:, t, :]))
                    link.join()
                    rsqrt(dve, link, ag[:, :, 1], rs_v[:], rs_y[:], rs_t[:], EPS)
                    wait(dve, f_full, after(n - 1, UF, F_AT["xt"]))
                    for t in range(QT):
                        dve.tensor_scalar(xn[:, t, :], xin[w][:, t, :], ag[:, t, 0:1], rs_y[:, t:t + 1], ALU.subtract, ALU.mult).then_inc(x_ln, 1)
                elif k in ("c1", "c3"):
                    i, (t0, cnt) = F_AT[k], TG[int(k[1])]
                    width = min(KEYS, (t0 + cnt) * P) - t0 * P
                    wait(dve, f_full, after(n, UF, i))
                    wait(dve, s_full, n * QT * NCH)
                    dve.tensor_copy(ct[:, t0 * P:t0 * P + width], fbank[i % 2][:, 0:width]).then_inc(f_done(n, i)[0], 1)
                elif k in ("s0", "s1"):
                    qt = int(k[1])
                    wait(dve, s_exp, after(n - 1, QT * NCH, QT * NCH - 1))
                    for c, (at, width) in enumerate(CH):
                        wait(dve, s_full, after(n, QT * NCH, qt * NCH + c))
                        dve.tensor_reduce(mx[:, qt, c:c + 1], sbank[c][:, 0:width], AX.X, ALU.max).then_inc(s_max, 1)
                    dve.wait_ge(s_max, after(n, QT * (NCH + 1), qt * (NCH + 1) + NCH - 1))
                    dve.tensor_reduce(nm[:, qt:qt + 1], mx[:, qt, :], AX.X, ALU.max, negate=True).then_inc(s_max, 1)
                    dve.wait_ge(s_max, after(n, QT * (NCH + 1), qt * (NCH + 1) + NCH))
                    dve.tensor_scalar(nm[:, qt:qt + 1], nm[:, qt:qt + 1], D ** -0.5, None, ALU.mult).then_inc(s_neg, 1)
                    dve.wait_ge(s_exp, after(n, QT * NCH, qt * NCH + NCH - 1))
                    dve.reduce_sum(tot[:, qt:qt + 1], sums[:, qt, :], AX.X).then_inc(s_sum, 1)
                    dve.wait_ge(s_sum, after(n, QT, qt))
                    wait(dve, s_norm, after(n - 1, QT, qt))
                    dve.reciprocal(rec[:, qt:qt + 1], tot[:, qt:qt + 1]).then_inc(s_rec, 1)
                elif k[0] == "p" and k != "pc" and int(k[2]) % 2:
                    move_probs(dve, dve.tensor_copy, k, n)

            def back(k, d, w):
                i = B_AT[k]
                src = gbank[i % 2]
                freed = b_done(d, i)[0]
                if k == "r":
                    link = Chain(dve, r_dve, d * R_PER)
                    wait(dve, b_full, after(d, UB, i))
                    wait(dve, *b_done(d - 1, B_AT["e1"]))
                    ins = dve.tensor_tensor(lg[:], src[:, 0:QT * EXPERTS].rearrange("p (t e) -> p t e", e=EXPERTS),
                                            rrow[w][:].unsqueeze(1).to_broadcast([P, QT, EXPERTS]), ALU.add)
                    ins.then_inc(freed, 1)
                    dve.wait_ge(*b_done(d, i))
                    link(dve.tensor_reduce(lm[:], lg[:], AX.X, ALU.max))
                    link.join()
                    link(dve.tensor_tensor(lx[:], lg[:], lm[:].unsqueeze(2).to_broadcast([P, QT, EXPERTS]), ALU.subtract))
                    link.join()
                    dve.wait_ge(r_exp, d + 1)
                    link(dve.reduce_sum(ls[:], le[:], AX.X))
                    link.join()
                    link(dve.reciprocal(ls[:], ls[:]))
                    link.join()
                    link(dve.tensor_tensor(rp[:], le[:], ls[:].unsqueeze(2).to_broadcast([P, QT, EXPERTS]), ALU.mult))
                    link.join()
                elif k in ("h0", "h1", "h2", "g1"):
                    h = {"h0": 0, "h1": 1, "h2": 2, "g1": 3}[k]
                    dve.wait_ge(h_tanh, after(d, 4, h))
                    if k == "g1":
                        wait(dve, b_full, after(d - 1, UB, B_AT["g2"]))
                        dve.scalar_tensor_tensor(out=g1[:], in0=gt[:], scalar=1.0, in1=gz[:], op0=ALU.add, op1=ALU.mult).then_inc(h_out, 1)
                    else:
                        wait(dve, b_full, after(d - 1, UB, B_AT["e1"]))
                        dve.scalar_tensor_tensor(out=hh[:, h].rearrange("p c n -> p (c n)"), in0=ht[:].rearrange("p c n -> p (c n)"), scalar=1.0,
                                                 in1=hz[:].rearrange("p c n -> p (c n)"), op0=ALU.add, op1=ALU.mult).then_inc(h_out, 1)
                elif k in ("e0", "e1"):
                    qt = int(k[1])
                    wait(dve, b_full, after(d, UB, i))
                    wait(dve, b_full, after(d - 1, UB, B_AT["rt"]))
                    base = d * QT * ACCS + qt * ACCS
                    for e in range(EXPERTS):
                        part = src[:, e * D:(e + 1) * D]
                        by = rp[:, qt, e:e + 1]
                        if e:
                            dve.wait_ge(r_acc, base + e)
                        else:
                            wait(dve, *(b_done(d, B_AT["e0"]) if qt else b_done(d - 1, B_AT["e1"])))
                        if e == 0:
                            ins = dve.tensor_scalar(acc[0][:], part, by, None, ALU.mult)
                        else:
                            ins = dve.scalar_tensor_tensor(out=acc[1][:] if e == 1 else rt[:, qt, :], in0=part, scalar=by, in1=acc[e - 1][:],
                                                           op0=ALU.mult, op1=ALU.add)
                        ins.then_inc(freed if e == EXPERTS - 1 else r_acc, 1)
                elif k == "g2":
                    dve.wait_ge(*b_done(d, i))
                    wait(dve, x_sum, d)
                    dve.tensor_scalar(g2[:], g2t[:], 0.5, 0.5, ALU.mult, ALU.add).then_inc(g_out, 1)
                elif k == "o":
                    wait(dve, b_full, after(d, UB, i))
                    dve.wait_ge(g_out, d + 1)
                    wait(dve, x_sum, d)
                    dve.tensor_tensor(y[:], src[:, 0:QT * D].rearrange("p (t d) -> p t d", d=D), g2[:], ALU.mult).then_inc(freed, 1)

            walk(dve, front, back)

        @block.scalar
        def _(act):
            act.wait_ge(consts, 16 * len(consts_list))

            def copy(dst, src):
                return act.activation(dst, src, ACT.Copy)

            def front(k, n, w):
                if k in F_AT:
                    i = F_AT[k]
                    src, freed = fbank[i % 2], f_done(n, i)[0]
                if k == "xt":
                    wait(act, f_full, after(n, UF, i))
                    wait(act, x_sum, n - 1)
                    act.activation(nxt[w][:], src[:, 0:NQ], ACT.Identity, bias=bet[:], scale=gam[:]).then_inc(freed, 1)
                elif k in ("q", "qk", "pc"):
                    wait(act, f_full, after(n, UF, i))
                    reader = {"q": after(n - 1, UF, F_AT["qk"]), "pc": after(n - 1, UF, F_AT["ev"])}
                    if k in reader:
                        wait(act, f_full, reader[k])
                    else:
                        wait(act, s_full, n * QT * NCH)
                    copy({"q": q, "qk": qk, "pc": pct}[k][:], src[:, 0:NQ]).then_inc(freed, 1)
                elif k == "ev":
                    wait(act, f_full, after(n, UF, i))
                    wait(act, x_sum, n - 1)
                    copy(evt[w][:], src[:, 0:NQ]).then_inc(freed, 1)
                elif k in ("c0", "c2"):
                    t0, cnt = TG[int(k[1])]
                    wait(act, f_full, after(n, UF, i))
                    wait(act, s_full, n * QT * NCH)
                    copy(ct[:, t0 * P:(t0 + cnt) * P], src[:, 0:cnt * P]).then_inc(freed, 1)
                elif k in ("s0", "s1"):
                    qt = int(k[1])
                    wait(act, s_neg, after(n, QT, qt))
                    wait(act, s_norm, after(n - 1, QT, qt))
                    for c, (at, width) in enumerate(CH):
                        act.activation(pr[qt][:, at:at + width], sbank[c][:, 0:width], ACT.Exp, bias=nm[:, qt:qt + 1], scale=D ** -0.5,
                                       accum_out=sums[:, qt, c:c + 1]).then_inc(s_exp, 1)
                elif k[0] == "p" and int(k[2]) % 2 == 0:
                    move_probs(act, copy, k, n)

            def back(k, d, w):
                i = B_AT[k]
                src, freed = gbank[i % 2], b_done(d, i)[0]
                if k == "r":
                    act.wait_ge(r_dve, d * R_PER + 2)
                    act.activation(le[:], lx[:], ACT.Exp).then_inc(r_exp, 1)
                elif k in ("h0", "h1", "h2", "g1"):
                    h = {"h0": 0, "h1": 1, "h2": 2, "g1": 3}[k]
                    wait(act, b_full, after(d, UB, i))
                    wait(act, h_out, after(d, 4, h - 1))
                    if k == "g1":
                        act.activation(gz[:], src[:, 0:NQ], ACT.Identity, bias=column(acols[w], L1_COLS + 6), scale=0.5).then_inc(freed, 1)
                        act.wait_ge(*b_done(d, i))
                        act.activation(gt[:], gz[:], ACT.Tanh).then_inc(h_tanh, 1)
                    else:
                        for c in range(2):
                            ins = act.activation(hz[:, c, :], src[:, c * NQ:(c + 1) * NQ], ACT.Identity, bias=column(acols[w], L1_COLS + 2 * h + c), scale=0.5)
                        ins.then_inc(freed, 1)
                        act.wait_ge(*b_done(d, i))
                        act.activation(ht[:], hz[:], ACT.Tanh).then_inc(h_tanh, 1)
                elif k == "g2":
                    wait(act, b_full, after(d, UB, i))
                    wait(act, g_out, d)
                    act.activation(g2t[:].rearrange("p t d -> p (t d)"), src[:, 0:QT * D], ACT.Tanh, scale=0.5).then_inc(freed, 1)
                elif k == "rt":
                    wait(act, b_full, after(d, UB, i))
                    wait(act, b_full, after(d - 1, UB, B_AT["o"]))
                    copy(rtt[:], src[:, 0:NQ]).then_inc(freed, 1)

            walk(act, front, back)

        @block.gpsimd
        def _(pool):
            def front(k, n, w):
                if k in ("s0", "s1"):
                    qt = int(k[1])
                    pool.wait_ge(s_rec, after(n, QT, qt))
                    wait_apart(pool, f_full, after(n - 1, UF, F_AT[f"p{qt}{len(TG) - 1}"]), (ready, 1))
                    pool.tensor_scalar(prn[qt][:], pr[qt][:], rec[:, qt:qt + 1], None, ALU.mult).then_inc(s_norm, 1)

            def back(k, d, w):
                if k == "o":
                    i = B_AT[k]
                    pool.wait_ge(*b_done(d, i))
                    wait(pool, x_out, 16 * d)
                    pool.tensor_tensor(xo[:], y[:], xin[w][:], ALU.add).then_inc(x_sum, 1)

            walk(pool, front, back)

        @block.tensor
        def _(pe):
            pe.wait_ge(consts, 16 * len(consts_list))
            pe.wait_ge(ready, 1)
            pe.transpose(gbank[0][:, 0:P], wk[:], ident[:]).then_inc(wk_turned, 1)
            pe.wait_ge(wk_turned, 2)

            def front(k, n, w):
                if k == "ln":
                    return
                if k in ("s0", "s1"):
                    qt = int(k[1])
                    wait(pe, *f_done(n, F_AT["qk"]))
                    for i in (F_AT["c2"], F_AT["c3"]):
                        wait(pe, *f_done(n, i))
                    for c, (at, width) in enumerate(CH):
                        wait(pe, s_exp, after(n, QT * NCH, (qt - 1) * NCH + c))
                        pe.matmul(sbank[c][:, 0:width], qk[:, qt * P:(qt + 1) * P], ct[:, at:at + width], start=True, stop=True).then_inc(s_full, 1)
                    return
                i = F_AT[k]
                dst = fbank[i % 2]
                bank_free(pe, f_done, n, i, UF)
                if k == "xt":
                    wait(pe, x_ln, (n + 1) * QT)
                    for t in range(QT):
                        ins = pe.transpose(dst[:, t * P:(t + 1) * P], xn[:, t, :], ident[:])
                elif k == "q":
                    wait(pe, *f_done(n, F_AT["xt"]))
                    ins = pe.matmul(dst[:, 0:NQ], wq[:], nxt[w][:], start=True, stop=True)
                elif k == "qk":
                    wait(pe, *f_done(n, F_AT["q"]))
                    ins = pe.matmul(dst[:, 0:NQ], wkt[:], q[:], start=True, stop=True)
                elif k[0] == "c":
                    t0, cnt = TG[int(k[1])]
                    wait(pe, c_in, (n + 1) * 32)
                    for t in range(t0, t0 + cnt):
                        rows = LAST if t == KT - 1 else P
                        ins = pe.transpose(dst[:, (t - t0) * P:(t - t0) * P + rows], cin[0:rows, t, :], ident[0:rows, 0:rows])
                elif k == "pc":
                    for j in range(F_AT["pc"] - 2, F_AT["pc"]):
                        wait(pe, *f_done(n, j))
                    for t in range(KT):
                        rows = LAST if t == KT - 1 else P
                        ins = pe.matmul(dst[:, 0:NQ], cin[0:rows, t, :], pt[0:rows, t].rearrange("p t q -> p (t q)"), start=(t == 0), stop=(t == KT - 1))
                elif k == "ev":
                    wait(pe, *f_done(n, F_AT["pc"]))
                    ins = pe.matmul(dst[:, 0:NQ], wv[:], pct[:], start=True, stop=True)
                else:
                    qt, g = int(k[1]), int(k[2])
                    t0, cnt = TG[g]
                    wait(pe, s_norm, after(n, QT, qt))
                    for t in range(t0, t0 + cnt):
                        rows = LAST if t == KT - 1 else P
                        ins = pe.transpose(dst[0:rows, (t - t0) * P:(t - t0 + 1) * P], prn[qt][:, t * P:t * P + rows], ident[:])
                ins.then_inc(f_full, 1)

            def back(k, d, w):
                i = B_AT[k]
                dst = gbank[i % 2]
                bank_free(pe, b_done, d, i, UB)
                if k == "r":
                    wait(pe, *f_done(d, F_AT["ev"]))
                    for t in range(QT):
                        for c, src in enumerate((nxt[w], evt[w])):
                            ins = pe.matmul(dst[:, t * EXPERTS:(t + 1) * EXPERTS], src[:, t * P:(t + 1) * P], rw[:, c, :], start=(c == 0), stop=(c == 1))
                elif k in ("h0", "h1", "h2"):
                    e = int(k[1])
                    for r in range(2):
                        for c, src in enumerate((nxt[w], evt[w])):
                            ins = pe.matmul(dst[:, r * NQ:(r + 1) * NQ], ew1[:, e, c, r * P:(r + 1) * P], src[:], start=(c == 0), stop=(c == 1))
                elif k == "g1":
                    for c, src in enumerate((nxt[w], evt[w])):
                        ins = pe.matmul(dst[:, 0:NQ], gw1[:, c, :], src[:], start=(c == 0), stop=(c == 1))
                elif k in ("e0", "e1"):
                    qt = int(k[1])
                    wait(pe, h_out, after(d, 4, 2))
                    for e in range(EXPERTS):
                        for r in range(2):
                            pe.matmul(dst[:, e * D:(e + 1) * D], hh[:, e, r, qt * P:(qt + 1) * P], ew2[:, e, r, :], start=(r == 0), stop=False)
                        ins = pe.matmul(dst[:, e * D:(e + 1) * D], ones[:], eb2[0:1, e, :], start=False, stop=True)
                elif k == "g2":
                    wait(pe, h_out, after(d, 4, 3))
                    for t in range(QT):
                        pe.matmul(dst[:, t * D:(t + 1) * D], g1[:, t * P:(t + 1) * P], gw2[:], start=True, stop=False)
                        ins = pe.matmul(dst[:, t * D:(t + 1) * D], ones[:], gb2[:], start=False, stop=True)
                elif k == "rt":
                    for key in ("e0", "e1"):
                        wait(pe, *b_done(d, B_AT[key]))
                    for t in range(QT):
                        ins = pe.transpose(dst[:, t * P:(t + 1) * P], rt[:, t, :], ident[:])
                elif k == "o":
                    wait(pe, *b_done(d, B_AT["rt"]))
                    for t in range(QT):
                        pe.matmul(dst[:, t * D:(t + 1) * D], rtt[:, t * P:(t + 1) * P], ow[:], start=True, stop=False)
                        ins = pe.matmul(dst[:, t * D:(t + 1) * D], ones[:], ob[:], start=False, stop=True)
                ins.then_inc(b_full, 1)

            walk(pe, front, back)


def layers(nc, a, out):
    def scratch(name, shape):
        return nc.dram_tensor(name, shape, F32, kind="Internal").ap()

    cols, rows = scratch("cond_cols", (B, P, N_COLS)), scratch("cond_rows", (B, N_ROWS, D))
    xs = [scratch(f"x_after_{i}", (B, NQ, D)) for i in range(5)]
    ident = a["ident"]
    w1 = {k: a[f"L1_xcond_{k}"] for k in ("gate_w1", "gate_b1", "gate_w2", "gate_b2", "e_w1", "e_b1", "e_w2", "e_b2", "out_w", "out_b", "router_b")}
    w1["router_w"] = a["L1_xcond_router_W"]
    modulation(nc, {**w1, "cond": a["cond_1024"], "w0": a["L0_xcond_W_mod"], "b0": a["L0_xcond_b_mod"],
                    "w3": a["L3_xcond_adaln_w"], "b3": a["L3_xcond_adaln_b"], "w2q": a["L2_xcond_Wss_q"], "b2q": a["L2_xcond_bss_q"],
                    "w2k": a["L2_xcond_Wss_kv"], "b2k": a["L2_xcond_bss_kv"]}, cols, rows, ident)

    def part(w, i):
        return w[:, i * D:(i + 1) * D] if len(w.shape) == 2 else w[i * D:(i + 1) * D]

    def own(prefix, name, x_src, x_dst, qkv, qkv_b, wo, bo, first_col, gate):
        w, b = a[prefix + qkv], a[prefix + qkv_b]
        attention_layer(nc, Attention(name, NQ, x_src, x_dst, part(w, 0), part(w, 1), part(w, 2), a[prefix + wo],
                                      part(b, 0), part(b, 1), part(b, 2), a[prefix + bo], 1e-6,
                                      q_cols=(first_col, first_col + 1), gate=gate), cols, rows, ident, B)

    def cross(prefix, name, x_src, x_dst, q, q_b, kv, kv_b, wo, bo, eps, ctx_ln, q_cols, k_cols, mlp):
        w, b = a[prefix + kv], a[prefix + kv_b]
        attention_layer(nc, Attention(name, S, x_src, x_dst, a[prefix + q], part(w, 0), part(w, 1), a[prefix + wo],
                                      a[prefix + q_b], part(b, 0), part(b, 1), a[prefix + bo], eps, ctx=a["ctx_1024"],
                                      ctx_ln=ctx_ln, q_cols=q_cols, k_cols=k_cols, mlp=mlp), cols, rows, ident, B)

    p0, p2, p3 = "L0_xcond_", "L2_xcond_", "L3_xcond_"
    own(p0, "l0_self", a["x"], xs[0], "W_qkv", "b_qkv", "W_proj", "b_proj", L0_COLS, 0)
    cross(p0, "l0_cross", xs[0], xs[1], "W_qc", "b_qc", "W_kvc", "b_kvc", "W_cproj", "b_cproj", 1e-6, 1e-6, None, None,
          dict(w1=a[p0 + "W_mlp1"], b1=a[p0 + "b_mlp1"], w2=a[p0 + "W_mlp2"], b2=a[p0 + "b_mlp2"],
               cols=(L0_COLS + 2, L0_COLS + 3), gate=1, eps=1e-6))
    expert_layer(nc, {**w1, "wq": a["L1_xcond_Wq"], "wk": a["L1_xcond_Wk"], "wv": a["L1_xcond_Wv"],
                      "gamma": a["L1_xcond_ln_gamma"], "beta": a["L1_xcond_ln_beta"]}, xs[1], xs[2], a["ctx_1024"], cols, rows, ident, B)
    cross(p2, "l2_cross", xs[2], xs[3], "Wq", "bq", "Wkv", "bkv", "Wp", "bp", 1e-5, 1e-5,
          (L2_COLS, L2_COLS + 1), (L2_COLS + 2, L2_COLS + 3), None)
    own(p3, "l3_self", xs[3], xs[4], "qkv_w", "qkv_b", "sa_proj_w", "sa_proj_b", L3_COLS, 2)
    cross(p3, "l3_cross", xs[4], out, "q_w", "q_b", "kv_w", "kv_b", "ca_proj_w", "ca_proj_b", 1e-6, None, None, None,
          dict(w1=a[p3 + "fc1_w"], b1=a[p3 + "fc1_b"], w2=a[p3 + "fc2_w"], b2=a[p3 + "fc2_b"],
               cols=(L3_COLS + 2, L3_COLS + 3), gate=3, eps=1e-6))


def kernel(**inputs):
    import numpy as _np
    import concourse.bacc as _bacc
    from concourse import mybir as _mybir
    from concourse.bass_utils import run_bass_kernel_spmd as _run

    nc = _bacc.Bacc("TRN2", target_bir_lowering=False, num_devices=1)
    arrays, args = {}, {}
    for name, value in {**inputs, "ident": _np.eye(128, dtype=_np.float32)}.items():
        array = _np.ascontiguousarray(value)
        arrays[f"in_{name}"] = array
        args[name] = nc.dram_tensor(f"in_{name}", array.shape, _mybir.dt.from_np(array.dtype), kind="ExternalInput").ap()
    out = nc.dram_tensor("out_x", (16, 256, 128), _mybir.dt.float32, kind="ExternalOutput").ap()
    layers(nc, args, out)
    return _run(nc, [arrays], core_ids=[0]).results[0]["out_x"]
```
